# Optimizing a Trainium2 kernel written in Bass

```python
import numpy as np
import jax
import jax.numpy as jnp

def _softmax(x, axis=-1):
    return jax.nn.softmax(x, axis=axis)
def _gelu(x):
    return jax.nn.gelu(x, approximate=True)
def _silu(x):
    return jax.nn.silu(x)
def _sigmoid(x):
    return jax.nn.sigmoid(x)
def _layernorm(x, axis=-1, eps=1e-5):
    m = jnp.mean(x, axis=axis, keepdims=True)
    v = jnp.var(x, axis=axis, keepdims=True)
    return (x - m) / jnp.sqrt(v + eps)
def _scatter_add(tgt, idx, src, axis=0):
    return tgt.at[idx].add(src)
def _segment_sum(src, seg, n):
    return jax.ops.segment_sum(src, seg, n)

kernel_name = 'mk_conv_seq_d2_conv_nchw256_8c8d96'

def setup_inputs(seed: int = 0):
    np.random.seed(seed)
    _w = jnp.asarray
    def _rec_inputs():
        import jax
        import jax.numpy as jnp
        _gk = jax.random.key(seed)
        x = -0.0002928 + 1 * jax.random.normal(jax.random.fold_in(_gk, 1), (4, 256, 64, 64), jnp.float32)
        return x
    x = _rec_inputs()
    def _L0_conv_setup():
        import jax, jax.numpy as jnp
        import numpy as np
        from jax import lax
        B, C, H, W = (4, 256, 64, 64)
        DN = ('NCHW', 'OIHW', 'NCHW')
        key = jax.random.key(seed)
        k1, k2, k3, k4, k5 = jax.random.split(key, 5)
        x = jax.random.normal(k1, (B, C, H, W), dtype=jnp.float32)
        w1 = jax.random.normal(k2, (128, C, 7, 7), dtype=jnp.float32) * 0.02
        b1 = jax.random.normal(k3, (128,), dtype=jnp.float32) * 0.02
        w2 = jax.random.normal(k4, (49, 128, 1, 1), dtype=jnp.float32) * 0.02
        b2 = jax.random.normal(k5, (49,), dtype=jnp.float32) * 0.02
        return {'x': x, 'w1': w1, 'b1': b1, 'w2': w2, 'b2': b2}
    _L0_conv_all = _L0_conv_setup()
    _L0_conv_in = {k: v for k, v in _L0_conv_all.items() if k in ('w1', 'b1', 'w2', 'b2', )}
    del _L0_conv_all

    def _L1_conv_setup():
        import jax, jax.numpy as jnp
        import numpy as np
        EPS = 1e-05

        def _conv(x, w, stride=1, pad=0):
            return jax.lax.conv_general_dilated(x, w, window_strides=(stride, stride), padding=[(pad, pad), (pad, pad)], dimension_numbers=('NCHW', 'OIHW', 'NCHW'))

        def _bn_train(x, gamma, beta):
            mean = x.mean(axis=(0, 2, 3), keepdims=True)
            var = x.var(axis=(0, 2, 3), keepdims=True)
            xn = (x - mean) * jax.lax.rsqrt(var + EPS)
            return gamma[None, :, None, None] * xn + beta[None, :, None, None]
        key = jax.random.key(seed)
        ks = jax.random.split(key, 4)
        N, Cin, H, W = (32, 256, 56, 56)
        mid = 64
        return {'x': jax.random.normal(ks[0], (N, Cin, H, W), jnp.float32), 'w1': jax.random.normal(ks[1], (mid, Cin, 1, 1), jnp.float32), 'g1': jnp.ones((mid,), jnp.float32), 'b1': jnp.zeros((mid,), jnp.float32), 'w2': jax.random.normal(ks[2], (mid, mid, 3, 3), jnp.float32), 'g2': jnp.ones((mid,), jnp.float32), 'b2': jnp.zeros((mid,), jnp.float32), 'w3': jax.random.normal(ks[3], (4 * mid, mid, 1, 1), jnp.float32), 'g3': jnp.ones((4 * mid,), jnp.float32), 'b3': jnp.zeros((4 * mid,), jnp.float32)}
    _L1_conv_all = _L1_conv_setup()
    _L1_conv_in = {k: v for k, v in _L1_conv_all.items() if k in ('w1', 'g1', 'b1', 'w2', 'g2', 'b2', 'w3', 'g3', 'b3', )}
    del _L1_conv_all

    return {
        "x": x,
        "L0_conv_w1": _L0_conv_in["w1"],
        "L0_conv_b1": _L0_conv_in["b1"],
        "L0_conv_w2": _L0_conv_in["w2"],
        "L0_conv_b2": _L0_conv_in["b2"],
        "L1_conv_w1": _L1_conv_in["w1"],
        "L1_conv_g1": _L1_conv_in["g1"],
        "L1_conv_b1": _L1_conv_in["b1"],
        "L1_conv_w2": _L1_conv_in["w2"],
        "L1_conv_g2": _L1_conv_in["g2"],
        "L1_conv_b2": _L1_conv_in["b2"],
        "L1_conv_w3": _L1_conv_in["w3"],
        "L1_conv_g3": _L1_conv_in["g3"],
        "L1_conv_b3": _L1_conv_in["b3"],
    }

def reference(x, L0_conv_w1, L0_conv_b1, L0_conv_w2, L0_conv_b2, L1_conv_w1, L1_conv_g1, L1_conv_b1, L1_conv_w2, L1_conv_g2, L1_conv_b2, L1_conv_w3, L1_conv_g3, L1_conv_b3):
    import jax
    import jax.numpy as jnp
    def _L0_conv_ref(x, w1, b1, w2, b2):
        import jax, jax.numpy as jnp
        import numpy as np
        from jax import lax
        B, C, H, W = (4, 256, 64, 64)
        DN = ('NCHW', 'OIHW', 'NCHW')
        k = lax.conv_general_dilated(x, w1, window_strides=(1, 1), padding=[(6, 6), (6, 6)], rhs_dilation=(2, 2), dimension_numbers=DN) + b1[None, :, None, None]
        k = lax.conv_general_dilated(k, w2, window_strides=(1, 1), padding=[(0, 0), (0, 0)], dimension_numbers=DN) + b2[None, :, None, None]
        attn = jax.nn.softmax(k, axis=1)
        xp = jnp.pad(x, ((0, 0), (0, 0), (6, 6), (6, 6)))
        shifts = jnp.stack([xp[:, :, 2 * u:2 * u + x.shape[2], 2 * v:2 * v + x.shape[3]] for u in range(7) for v in range(7)], axis=1)
        return jnp.einsum('bkchw,bkhw->bchw', shifts, attn)

    def _L1_conv_ref(x, w1, g1, b1, w2, g2, b2, w3, g3, b3):
        import jax, jax.numpy as jnp
        import numpy as np
        EPS = 1e-05

        def _conv(x, w, stride=1, pad=0):
            return jax.lax.conv_general_dilated(x, w, window_strides=(stride, stride), padding=[(pad, pad), (pad, pad)], dimension_numbers=('NCHW', 'OIHW', 'NCHW'))

        def _bn_train(x, gamma, beta):
            mean = x.mean(axis=(0, 2, 3), keepdims=True)
            var = x.var(axis=(0, 2, 3), keepdims=True)
            xn = (x - mean) * jax.lax.rsqrt(var + EPS)
            return gamma[None, :, None, None] * xn + beta[None, :, None, None]
        residual = x
        h = jax.nn.relu(_bn_train(_conv(x, w1, 1, 0), g1, b1))
        h = jax.nn.relu(_bn_train(_conv(h, w2, 1, 1), g2, b2))
        h = _bn_train(_conv(h, w3, 1, 0), g3, b3)
        return jax.nn.relu(h + residual)

    def _gn(v, G=32, eps=1e-5):
        B_, C_, H_, W_ = v.shape
        g = v.reshape(B_, G, C_ // G, H_, W_)
        m = jnp.mean(g, axis=(2, 3, 4), keepdims=True)
        s = jnp.var(g, axis=(2, 3, 4), keepdims=True)
        return ((g - m) / jnp.sqrt(s + eps)).reshape(v.shape)

    def _ln_c(v, eps=1e-6):
        m = jnp.mean(v, axis=1, keepdims=True)
        s = jnp.var(v, axis=1, keepdims=True)
        return (v - m) / jnp.sqrt(s + eps)

    def _ln_t(v, eps=1e-5):
        m = jnp.mean(v, axis=-1, keepdims=True)
        s = jnp.var(v, axis=-1, keepdims=True)
        return (v - m) / jnp.sqrt(s + eps)

    def _to_tokens(v):
        B_, C_, H_, W_ = v.shape
        return v.reshape(B_, C_, H_ * W_).transpose(0, 2, 1)
    def _from_tokens(t, like):
        B_, C_, H_, W_ = like.shape
        return t.transpose(0, 2, 1).reshape(B_, C_, H_, W_)

    x = _L0_conv_ref(x, L0_conv_w1, L0_conv_b1, L0_conv_w2, L0_conv_b2)
    x = _L1_conv_ref(x, L1_conv_w1, L1_conv_g1, L1_conv_b1, L1_conv_w2, L1_conv_g2, L1_conv_b2, L1_conv_w3, L1_conv_g3, L1_conv_b3)
    return x


_drawn_inputs = setup_inputs


def setup_inputs(seed=0):
    import zlib

    import numpy as np

    out = dict(_drawn_inputs(seed))
    spreads = {'L1_conv_g1': (1.0, 0.2),
     'L1_conv_b1': (0.0, 0.1),
     'L1_conv_g2': (1.0, 0.2),
     'L1_conv_b2': (0.0, 0.1),
     'L1_conv_g3': (1.0, 0.2),
     'L1_conv_b3': (0.0, 0.1)}
    factors = {'L0_conv_b1': 8.0}
    for name, (base, spread) in spreads.items():
        noise = np.random.default_rng([zlib.crc32(name.encode()), seed]).standard_normal(out[name].shape)
        drawn = base * np.exp(spread * noise) if base else spread * noise
        out[name] = jnp.asarray(drawn.astype(out[name].dtype))
    for name, factor in factors.items():
        out[name] = (out[name] * factor).astype(out[name].dtype)
    return out
```

```python
from contextlib import ExitStack

import numpy as np

import concourse.bass as bass
from concourse import mybir

F32 = mybir.dt.float32
F32R = mybir.dt.float32r
U32 = mybir.dt.uint32
ALU = mybir.AluOpType
ACT = mybir.ActivationFunctionType
AX_X = mybir.AxisListType.X

P = 128
B, C, H, W = 4, 256, 64, 64
CB = C // P
K = 7
KK = K * K
MID0 = 128
SH, SW = H // 2, W // 2
SPX = SH * SW
HALF = SPX // 2
HR = SH // 2
PAD = K // 2
PW = SW + 2 * PAD
PH = SH + 2 * PAD
PLANE = PH * PW
UPLANES = K * (PLANE - 1) + PW
PLANES = (2 * K - 1) * UPLANES
UK = K * KK
MB = 115
MS = [MB, MB, UK - 2 * MB]
NT = SH // 4
WIN = 4 + 2 * PAD
JV = WIN * K
MID1 = 64
STEPS = 4 * B
EPS = 1e-5
SELB = KK
SELW = SELB + MB + KK
LAG = 3


def window(h, t):
    return max(4 * t - PAD, HR * h), min(4 * t + 4 + PAD, HR * h + HR)


TILES = [[t for t in range(NT) if window(h, t)[0] < window(h, t)[1]] for h in range(2)]
UNITS = [(h, t) for h in range(2) for t in TILES[h]]


def build(nc, x, w1, b1, w2, b2, v1, g1, c1, v2, g2, c2, v3, g3, c3, out):
    attn_planes = nc.dram_tensor("attn_planes", (2, PLANES), F32, kind="Internal").ap()
    x1_dram = nc.dram_tensor("x1_dram", (STEPS, CB, P, SPX), F32, kind="Internal").ap()
    y1_dram = nc.dram_tensor("y1_dram", (STEPS, MID1, SPX), F32, kind="Internal").ap()

    top = ExitStack()
    with top:
        def sem(name):
            return top.enter_context(nc.semaphore(name))

        def sb(stack, name, shape, dt=F32):
            return stack.enter_context(nc.sbuf_tensor(name, shape, dt))

        ps = top.enter_context(nc.psum_tensor("ps", [P, 8, 512], F32))
        psR = [ps[:, 0, :], ps[:, 1, :]]
        psX = [ps[:, 2, :], ps[:, 3, :]]
        psU, psT, psXT, psB = ps[:, 4, :], ps[:, 5, :], ps[:, 6, :], ps[:, 7, :]

        ident = sb(top, "ident", [P, P])
        gavg = sb(top, "gavg", [P, P])
        v3raw = sb(top, "v3raw", [P, CB, 2, MID1])
        v2raw = sb(top, "v2raw", [MID1, 2, MID1 * 9])
        bn = sb(top, "bn", [P, 8])

        l0 = ExitStack()
        w_hi = sb(l0, "w_hi", [P, CB, K, UK], F32R)
        w_lo = sb(l0, "w_lo", [P, CB, K, UK], F32R)
        xraw = sb(l0, "xraw", [P, CB, SH, W])
        xs_hi = sb(l0, "xs_hi", [P, 2, CB, SH, PW], F32R)
        xs_lo = sb(l0, "xs_lo", [P, 2, CB, SH, PW], F32R)
        self32 = sb(l0, "self32", [P, SELW])
        sel = sb(l0, "sel", [P, SELW], F32R)
        mask = sb(l0, "mask", [P, K, SW])
        v1pack = sb(l0, "v1pack", [P, CB, P], F32R)
        band = sb(l0, "band", [P, 2, WIN, SW])
        attn_pad = sb(l0, "attn_pad", [KK, PH, PW])
        beff = sb(l0, "beff", [KK, 1])
        w2T = sb(l0, "w2T", [P, KK])
        b1s = sb(l0, "b1s", [P, 1])
        b2s = sb(l0, "b2s", [KK, 1])
        l0a = ExitStack()
        w1raw = sb(l0a, "w1raw", [P, CB, P, KK])
        w2raw = sb(l0a, "w2raw", [KK, P])
        v1raw = sb(l0a, "v1raw", [MID1, C])
        zeros = sb(l0a, "zeros", [P, 1024])
        l0a.close()
        l0b = ExitStack()
        r_hi = sb(l0b, "r_hi", [P, 3, SPX], F32R)
        r_lo = sb(l0b, "r_lo", [P, 3, SPX], F32R)
        logits = sb(l0b, "logits", [KK, SPX])
        expo = sb(l0b, "expo", [P, NT, KK])
        probs = sb(l0b, "probs", [P, NT, KK])
        smx = sb(l0b, "smx", [P, 3, NT])
        attn_jv = sb(l0b, "attn_jv", [JV, NT, P])
        xq = sb(l0b, "xq", [P, CB, SH, W])
        xT_hi = sb(l0b, "xT_hi", [P, 4, C], F32R)
        xT_lo = sb(l0b, "xT_lo", [P, 4, C], F32R)
        band_hi = sb(l0b, "band_hi", [P, 4, WIN, SW], F32R)
        band_lo = sb(l0b, "band_lo", [P, 4, WIN, SW], F32R)
        x1 = sb(l0b, "x1", [P, CB, 2, HALF])
        x1_hi = sb(l0b, "x1_hi", [P, CB, 2, HALF], F32R)
        x1_lo = sb(l0b, "x1_lo", [P, CB, 2, HALF], F32R)
        y1half = sb(l0b, "y1half", [MID1, HALF])
        y1 = sb(l0b, "y1", [MID1, 2, HALF])
        l0b.close()
        l0.close()

        l1 = ExitStack()
        y = sb(l1, "y", [P, 8, SPX])
        v2_hi = sb(l1, "v2_hi", [P, 9, P], F32R)
        v2_lo = sb(l1, "v2_lo", [P, 9, P], F32R)
        v3_hi = sb(l1, "v3_hi", [P, 2, C], F32R)
        v3_lo = sb(l1, "v3_lo", [P, 2, C], F32R)
        stats = sb(l1, "stats", [P, 16, 6])
        stats3 = sb(l1, "stats3", [P, CB, 32, 6])
        mv = sb(l1, "mv", [P, 16])
        scale = sb(l1, "scale", [P, 4])
        shift = sb(l1, "shift", [P, 4])
        h2_hi = sb(l1, "h2_hi", [P, 8, SPX], F32R)
        h2_lo = sb(l1, "h2_lo", [P, 8, SPX], F32R)
        l1a = ExitStack()
        h1_hi = sb(l1a, "h1_hi", [P, 2, 4, SH + 2, SW + 2], F32R)
        h1_lo = sb(l1a, "h1_lo", [P, 2, 4, SH + 2, SW + 2], F32R)
        l1a.close()
        l1b = ExitStack()
        x1in = sb(l1b, "x1in", [P, 2, 4, SPX])
        outs = sb(l1b, "outs", [P, 2, H, W])
        l1b.close()
        l1.close()

        zeroed, consts, masked, sel_ready = sem("zeroed"), sem("consts"), sem("masked"), sem("sel_ready")
        small_loaded, bn_loaded, w1_loaded = sem("small_loaded"), sem("bn_loaded"), [sem("w1_loaded0"), sem("w1_loaded1")]
        planes_zero = sem("planes_zero")
        prep_pe, prep_dve = sem("prep_pe"), sem("prep_dve")
        weff_done, whi_done, wlo_done = sem("weff_done"), sem("whi_done"), sem("wlo_done")
        x_loaded, xs_hi_done, xs_lo_done = sem("x_loaded"), sem("xs_hi_done"), sem("xs_lo_done")
        group_done, r_hi_done, r_lo_done = sem("group_done"), sem("r_hi_done"), sem("r_lo_done")
        usum_done, logits_done, lt_done = sem("usum_done"), sem("logits_done"), sem("lt_done")
        max_done, sub_done, exp_done = sem("max_done"), sem("sub_done"), sem("exp_done")
        norm_done, probs_done = sem("norm_done"), sem("probs_done")
        at_done, attn_done, attn_stored, attn_loaded = sem("at_done"), sem("attn_done"), sem("attn_stored"), sem("attn_loaded")
        bt_done, band_step, band_hi_done, band_lo_done = sem("bt_done"), sem("band_step"), sem("band_hi_done"), sem("band_lo_done")
        xq_loaded = [sem("xq_loaded0"), sem("xq_loaded1")]
        xt_done, xT_hi_done, xT_lo_done = sem("xt_done"), sem("xT_hi_done"), sem("xT_lo_done")
        unit_done, x1_hi_done, x1_done, x1_lo_done = sem("unit_done"), sem("x1_hi_done"), sem("x1_done"), sem("x1_lo_done")
        y_done, yhalf_done, y1_done = sem("y_done"), sem("yhalf_done"), sem("y1_done")
        x1_stored, y1_stored = [sem("x1_stored0"), sem("x1_stored1")], sem("y1_stored")
        y_loaded, borders, vt_done, v_hi_done, v_lo_done = sem("y_loaded"), sem("borders"), sem("vt_done"), sem("v_hi_done"), sem("v_lo_done")
        y_stat = sem("y_stat")
        dve_gate, pe_gate, sp_gate = sem("dve_gate"), sem("pe_gate"), sem("sp_gate")
        bn_dve, bn_pe, bn_act = sem("bn_dve"), sem("bn_pe"), sem("bn_act")
        relu1, h1_hi_done, h1_lo_done = sem("relu1"), sem("h1_hi_done"), sem("h1_lo_done")
        relu2, h2_hi_done, h2_lo_done = sem("relu2"), sem("h2_hi_done"), sem("h2_lo_done")
        c2_done, c2_copied, c2_stat = sem("c2_done"), sem("c2_copied"), sem("c2_stat")
        c3_done, c3_stat = sem("c3_done"), sem("c3_stat")
        f_done, f_added, f_out = sem("f_done"), sem("f_added"), sem("f_out")
        x1_back = [sem("x1_back0"), sem("x1_back1")]
        out_stored = [sem("out_stored0"), sem("out_stored1")]

        class Step:

            def __init__(self, n, q, back=0):
                self.n, self.q, self.back = n, q, back
                self.k = q - back
                self.b = self.k % 2
                self.a = (self.k // 2) % 2

            def live(self, ago=0):
                return not isinstance(self.n, int) or 0 <= 4 * self.n + self.k - ago < STEPS

            def count(self, per_step, i):
                return self.n * (4 * per_step) + (self.k * per_step + i + 1)

            def dma(self, per_step, i):
                return self.n * (64 * per_step) + 16 * (self.k * per_step + i + 1)

            def index(self):
                return self.n * 4 + self.k

            def image(self):
                return self.n + self.k // 4

            def ago(self, m):
                return Step(self.n, self.q, self.back + m)

        def each_step(eng, step):
            for q in range(4):
                step(0, q)
            with eng.Fori(1, B) as n:
                for q in range(4):
                    step(n, q)
            for q in range(LAG):
                step(B, q)

        def main_live(n):
            return not isinstance(n, int) or n < B

        block = top.enter_context(nc.Block())

        def store_out(sp, u):
            n2, g, cb = u // 4, (u // 2) % 2, u % 2
            for h in range(2):
                sp.wait_ge(f_out, 8 * u + 4 * h + 4)
                sp.dma_start(out[2 * g + n2, cb * P:(cb + 1) * P, 32 * h:32 * h + 32, :],
                             outs[:, u % 2, 32 * h:32 * h + 32, :]).then_inc(out_stored[u % 2], 16)

        def load_rows(sp, dst, n, a, done, r0=0, r1=SH):
            for cb in range(CB):
                src = x[n, cb * P:(cb + 1) * P].rearrange("p (r a) w -> p r a w", a=2)[:, r0:r1, a, :]
                sp.dma_start(dst[:, cb, r0:r1, :], src).then_inc(done, 16)

        def last_unit(t):
            return max(i for i, (h, tt) in enumerate(UNITS) if tt == t)

        def wait_slot(eng, p, t):
            if t >= 4:
                eng.wait_ge(unit_done, p.count(len(UNITS), last_unit(t - 4)))
            elif p.live(1):
                eng.wait_ge(unit_done, p.ago(1).count(len(UNITS), last_unit(t + 4)))

        @block.sync
        def _(sp):
            sp.dma_start(w2raw[:, :], w2.rearrange("k o a b -> k (o a b)")).then_inc(small_loaded, 16)
            sp.dma_start(v1raw[:, :], v1.rearrange("m c a b -> m (c a b)")).then_inc(small_loaded, 16)
            sp.dma_start(b1s[:, :], b1.rearrange("(p a) -> p a", a=1)).then_inc(small_loaded, 16)
            sp.dma_start(b2s[:, :], b2.rearrange("(p a) -> p a", a=1)).then_inc(small_loaded, 16)
            for kb in range(CB):
                sp.dma_start(w1raw[:, kb, :, :].rearrange("p c t -> p (c t)"),
                             w1[:, kb * P:(kb + 1) * P, :, :].rearrange("o c u v -> o (c u v)")
                             ).then_inc(w1_loaded[kb], 16)
                if kb == 0:
                    load_rows(sp, xraw, 0, 0, x_loaded)
            sp.wait_ge(zeroed, 1)
            total = 2 * PLANES
            flat = attn_planes.rearrange("s e -> (s e)")
            whole = total // (P * 1024)
            for i in range(whole):
                sp.dma_start(flat[i * P * 1024:(i + 1) * P * 1024].rearrange("(p e) -> p e", p=P),
                             zeros[:, :]).then_inc(planes_zero, 16)
            rest = total - whole * P * 1024
            rows = rest // 1024
            sp.dma_start(flat[whole * P * 1024:(whole * P + rows) * 1024].rearrange("(p e) -> p e", p=rows),
                         zeros[0:rows, :]).then_inc(planes_zero, 16)
            tail = rest - rows * 1024
            if tail:
                sp.dma_start(flat[total - tail:total].rearrange("(p e) -> p e", p=1),
                             zeros[0:1, 0:tail]).then_inc(planes_zero, 16)
            for g in range(2):
                for i, t in enumerate((g1, c1, g2, c2)):
                    sp.dma_start(bn[64 * g:64 * g + 64, i:i + 1], t.rearrange("(p a) -> p a", a=1)).then_inc(bn_loaded, 16)
                sp.dma_start(v3raw[:, :, g, :], v3.rearrange("(b p) m x y -> p b (m x y)", p=P)).then_inc(bn_loaded, 16)
                sp.dma_start(v2raw[:, g, :], v2.rearrange("o i y x -> o (i y x)")).then_inc(bn_loaded, 16)
            for i, t in enumerate((g3, c3)):
                for cb in range(CB):
                    sp.dma_start(bn[:, 4 + 2 * i + cb:5 + 2 * i + cb],
                                 t[cb * P:(cb + 1) * P].rearrange("(p a) -> p a", a=1)).then_inc(bn_loaded, 16)
            sp.wait_ge(planes_zero, 16 * (whole + 1 + bool(tail)))

            def step(n, q):
                s, p1, p2, p3 = (Step(n, q, d) for d in range(4))
                at3, at2, following = p3.index(), p2.index(), (n + 1) % B
                if not isinstance(n, int):
                    at3, at2 = sp.snap(at3), sp.snap(at2)
                    following = sp.snap(following) if q == 2 else None
                if p3.live():
                    sp.wait_ge(x1_done, p3.count(4, 3))
                    store_x1(at3, 1)
                if q % 2 == 0 and main_live(n):
                    sp.wait_ge(xs_hi_done, s.count(2, 3))
                    sp.wait_ge(xs_lo_done, s.count(2, 3))
                    if q == 0:
                        load_rows(sp, xraw, n, 1, x_loaded)
                    else:
                        load_rows(sp, xraw, following, 0, x_loaded)
                if q % 2 == 1 and main_live(n):
                    load_xq(n, s, p2, 0)
                if p3.live():
                    sp.wait_ge(y1_done, p3.count(2, 1))
                    sp.dma_start(y1_dram[at3], y1[:, :, :].rearrange("m h e -> m (h e)")).then_inc(y1_stored, 16)
                if p1.live():
                    sp.wait_ge(attn_done, p1.count(2, 1))
                    sp.sem_inc(sp_gate, 1)
                    if p1.live(2):
                        sp.wait_ge(attn_loaded, p1.ago(2).dma(NT, NT - 1))
                    sp.dma_start(bass.AP(tensor=attn_planes.tensor, offset=p1.b * PLANES + PAD * UPLANES,
                                         ap=[[UPLANES, K], [PLANE, K], [1, PLANE]]),
                                 attn_pad[:, :, :].rearrange("k r c -> k (r c)")).then_inc(attn_stored, 16)
                if p2.live():
                    sp.wait_ge(x1_done, p2.count(4, 1))
                    store_x1(at2, 0)
                if p1.live():
                    sp.wait_ge(attn_stored, p1.dma(1, 0))
                    sp.sem_inc(sp_gate, 1)
                    if p1.live(1):
                        sp.wait_ge(bt_done, p2.count(2, 1))
                    for t in range(NT):
                        src = bass.AP(tensor=attn_planes.tensor,
                                      offset=p1.b * PLANES + (4 * t + WIN - 1) * PW + 2 * PAD,
                                      ap=[[PLANE - 1, JV], [UPLANES, 4], [1, SW]])
                        sp.dma_start(attn_jv[:, t, :], src).then_inc(attn_loaded, 16)
                if q % 2 == 1 and main_live(n):
                    load_xq(n, s, p2, 1)

            def store_x1(at, h):
                sp.dma_start(x1_dram[at][:, :, h * HALF:(h + 1) * HALF].rearrange("b p e -> p b e"),
                             x1[:, :, h, :]).then_inc(x1_stored[h], 16)

            def load_xq(n, s, p2, half):
                if p2.live():
                    sp.wait_ge(xt_done, p2.count(4, 1 if half == 0 else 3))
                    sp.sem_inc(sp_gate, 1)
                else:
                    sp.wait_ge(group_done, 1)
                load_rows(sp, xq, n, s.a, xq_loaded[half], half * HR, half * HR + HR)

            each_step(sp, step)

            sp.wait_ge(y1_stored, 16 * STEPS)
            for h in range(2):
                sp.wait_ge(x1_stored[h], 16 * STEPS)
            for i in range(8):
                for g in range(2):
                    sp.dma_start(y[64 * g:64 * g + 64, i, :], y1_dram[8 * g + i]).then_inc(y_loaded, 16)
            sp.wait_ge(c2_done, 16)
            for u in range(8):
                n2, g, cb = u // 4, (u // 2) % 2, u % 2
                if u >= 2:
                    sp.wait_ge(f_out, 8 * (u - 1))
                s0 = 8 * g + 4 * n2
                sp.dma_start(x1in[:, u % 2, :, :], x1_dram[s0:s0 + 4, cb].rearrange("s p e -> p s e")
                             ).then_inc(x1_back[u % 2], 16)
                if u >= 1:
                    store_out(sp, u - 1)
            store_out(sp, 7)
            for k in range(2):
                sp.wait_ge(out_stored[k], 16 * 8)

        @block.gpsimd
        def _(pool):
            pool.memset(zeros[:, :], 0.0).then_inc(zeroed, 1)
            for t in (ident[:, :], gavg[:, :], self32[:, :], mask[:, :, :]):
                pool.memset(t, 0.0).then_inc(consts, 1)
            for t in (xs_hi, xs_lo):
                for b in range(2):
                    for c0 in (0, PAD + SW):
                        pool.memset(t[:, b, :, :, c0:c0 + PAD].bitcast(F32), 0.0).then_inc(consts, 1)
            pool.memset(band[:, :, :, :], 0.0).then_inc(consts, 1)
            pool.memset(attn_pad[:, :, :], 0.0).then_inc(consts, 1)
            pool.wait_ge(consts, 14)

            puts = [(ident[:, :], 1.0, 0, [[-1, P]], 1), (gavg[:, :], 0.5, 0, [[-1, P]], 1),
                    (self32[:, :], 1.0, -SELB, [[1, SELW]], -1)]
            puts += [(mask[32 * g:32 * g + 32, :, :], 1.0, -PAD, [[1, K], [1, SW]], -1) for g in range(4)]
            puts += [(gavg[:, :], 0.5, d, [[-1, P]], 1) for d in (64, -64)]
            for i, (t, value, base, pattern, per_partition) in enumerate(puts):
                if i:
                    pool.wait_ge(masked, i)
                pool.affine_select(out=t, in_=t, compare_op=ALU.not_equal, fill=value, base=base, pattern=pattern,
                                   channel_multiplier=per_partition).then_inc(masked, 1)
            pool.wait_ge(masked, len(puts))

            def split_lo(s):
                for kb in range(CB):
                    pool.wait_ge(xs_hi_done, s.count(2, kb))
                    pool.tensor_tensor(xs_lo[:, s.b, kb, :, PAD:PAD + SW], xraw[:, kb, :, s.b::2],
                                       xs_hi[:, s.b, kb, :, PAD:PAD + SW].bitcast(F32), ALU.subtract
                                       ).then_inc(xs_lo_done, 1)

            split_lo(Step(0, 0))

            def step(n, q):
                s, p1, p2, p3 = (Step(n, q, d) for d in range(4))
                nxt = Step(n, q, -1)
                for t in range(NT):
                    if p2.live():
                        pool.wait_ge(band_hi_done, p2.count(NT, t))
                        wait_slot(pool, p2, t)
                        pool.tensor_tensor(band_lo[:, t % 4, :, :], band[:, t % 2, :, :],
                                           band_hi[:, t % 4, :, :].bitcast(F32), ALU.subtract
                                           ).then_inc(band_lo_done, 1)
                    if t == 1 and main_live(n):
                        if s.live(1):
                            pool.wait_ge(group_done, p1.count(6, 5))
                        split_lo(nxt)

            each_step(pool, step)

            pool.wait_ge(y1_done, 2 * STEPS)
            pool.wait_ge(unit_done, len(UNITS) * STEPS)
            for h in range(2):
                pool.wait_ge(x1_stored[h], 16 * STEPS)
            pool.wait_ge(y1_stored, 16 * STEPS)
            for t in (h1_hi, h1_lo):
                for e in (0, SH + 1):
                    pool.memset(t[:, :, :, e, :].bitcast(F32), 0.0).then_inc(borders, 1)
                    pool.memset(t[:, :, :, 1:SH + 1, e:e + 1].bitcast(F32), 0.0).then_inc(borders, 1)
            for t in (v2_hi, v2_lo, v3_hi, v3_lo):
                pool.memset(t[:, :, :].bitcast(F32), 0.0).then_inc(borders, 1)

        @block.scalar
        def _(act):
            def copy(dst, src):
                return act.activation(dst, src, ACT.Copy)

            act.wait_ge(prep_pe, 3)
            for kb in range(CB):
                copy(v1pack[:, kb, 0:MID1], psT[:, kb * MID1:(kb + 1) * MID1]).then_inc(whi_done, 1)
            act.wait_ge(masked, 7)
            copy(sel[:, :], self32[:, :]).then_inc(sel_ready, 1)
            act.wait_ge(consts, 14)

            def split_hi(s, which):
                for kb in which:
                    copy(xs_hi[:, s.b, kb, :, PAD:PAD + SW], xraw[:, kb, :, s.b::2]).then_inc(xs_hi_done, 1)

            act.wait_ge(x_loaded, 32)
            split_hi(Step(0, 0), range(CB))
            for i in range(CB * K):
                kb, v = i // K, i % K
                act.wait_ge(weff_done, i + 1)
                copy(w_hi[:, kb, v, :], psR[i % 2][:, 0:UK]).then_inc(whi_done, 1)

            def step(n, q):
                s, p1, p2, p3 = (Step(n, q, d) for d in range(4))
                nxt = Step(n, q, -1)

                def x_out(p, h):
                    for cb in range(CB):
                        if cb == 0:
                            act.wait_ge(unit_done, p.count(len(UNITS), 4 if h == 0 else 9))
                            if p.live(1):
                                act.wait_ge(y_done, p.ago(1).count(2, h))
                        copy(x1_hi[:, cb, h, :], psX[cb]).then_inc(x1_hi_done, 1)
                    if p.live(1):
                        act.wait_ge(x1_stored[h], p.ago(1).dma(1, 0))
                    for cb in range(CB):
                        copy(x1[:, cb, h, :], psX[cb]).then_inc(x1_done, 1)

                def logit(h):
                    act.wait_ge(usum_done, p1.count(2, h))
                    if p1.live(1) and h == 0:
                        act.wait_ge(lt_done, p2.count(1, 0))
                    act.activation(logits[:, h * HALF:(h + 1) * HALF], (psU if h == 0 else psT)[0:KK, :],
                                   ACT.Identity, bias=beff[:, 0:1]).then_inc(logits_done, 1)

                def xT(pair):
                    t = 2 * pair
                    act.wait_ge(xt_done, p2.count(4, pair))
                    wait_slot(act, p2, t + 1)
                    copy(xT_hi[:, t % 4:t % 4 + 2, :], psXT.rearrange("p (t c) -> p t c", c=C)).then_inc(xT_hi_done, 1)

                def bandhi(t):
                    act.wait_ge(band_step, p2.count(NT * K, t * K + K - 1))
                    wait_slot(act, p2, t)
                    copy(band_hi[:, t % 4, :, :], band[:, t % 2, :, :]).then_inc(band_hi_done, 1)

                def rhi(g):
                    h, m = g // 3, g % 3
                    act.wait_ge(group_done, s.count(6, g))
                    if p1.live():
                        act.wait_ge(usum_done, p1.count(2, 1))
                    copy(r_hi[0:MS[m], m, h * HALF:(h + 1) * HALF], psR[g % 2][0:MS[m], :]).then_inc(r_hi_done, 1)

                def attn(h):
                    act.wait_ge(at_done, p1.count(2, h))
                    if h == 0 and p1.live(1):
                        act.wait_ge(attn_stored, p2.dma(1, 0))
                    src = (psT if h == 0 else psU)[0:KK, :].rearrange("k (r c) -> k r c", c=SW)
                    copy(attn_pad[:, PAD + HR * h:PAD + HR * (h + 1), PAD:PAD + SW], src).then_inc(attn_done, 1)

                def yhalf(p, h):
                    act.wait_ge(y_done, p.count(2, h))
                    if h == 1 or p.live(1):
                        act.wait_ge(y1_done, p.count(2, h) - 1)
                    copy(y1half[:, :], psU[MID1:P, :]).then_inc(yhalf_done, 1)

                main, two, one, three = main_live(n), p2.live(), p1.live(), p3.live()
                if three:
                    x_out(p3, 1)
                if two:
                    xT(0)
                if one:
                    logit(0)
                if two:
                    bandhi(0)
                if one:
                    logit(1)
                if main:
                    rhi(0)
                if two:
                    bandhi(1), xT(1)
                if main:
                    if p1.live():
                        act.wait_ge(group_done, p1.count(6, 5))
                    if q % 2 == 1:
                        act.wait_ge(x_loaded, n * 64 + 32 * ((q + 1) // 2 + 1))
                    split_hi(nxt, [0])
                if two:
                    bandhi(2)
                if main:
                    rhi(1)
                    split_hi(nxt, [1])
                if one:
                    act.wait_ge(sub_done, p1.count(1, 0))
                    act.activation(expo[:, :, :], expo[:, :, :], ACT.Exp).then_inc(exp_done, 1)
                if three:
                    yhalf(p3, 1)
                if two:
                    bandhi(3), xT(2)
                if one:
                    attn(0)
                if two:
                    bandhi(4)
                if main:
                    rhi(2)
                if one:
                    attn(1)
                if two:
                    bandhi(5)
                    x_out(p2, 0)
                if main:
                    rhi(3)
                if two:
                    bandhi(6)
                    xT(3)
                    yhalf(p2, 0)
                if main:
                    rhi(4)
                if two:
                    bandhi(7)
                if main:
                    rhi(5)

            each_step(act, step)

            act.wait_ge(borders, 12)
            for t in range(9):
                act.wait_ge(vt_done, t + 1)
                for g in range(2):
                    rows = slice(64 * g, 64 * g + 64)
                    copy(v2_hi[rows, t, rows], ps[rows, t % 8, 0:MID1]).then_inc(v_hi_done, 1)
            for cb in range(CB):
                act.wait_ge(vt_done, 10 + cb)
                for g in range(2):
                    rows = slice(64 * g, 64 * g + 64)
                    copy(v3_hi[rows, g, cb * P:(cb + 1) * P], ps[rows, 1 + cb, 0:P]).then_inc(v_hi_done, 1)

            def root(i, k):
                act.wait_ge(bn_dve, k)
                act.activation(mv[:, 8:10], mv[:, 6:8], ACT.Sqrt).then_inc(bn_act, 1)

            root(1, BN1_ROOT)
            act.wait_ge(bn_dve, BN1_END)
            for i in range(8):
                act.activation(y[:, i, :], y[:, i, :], ACT.Relu, bias=shift[:, 0:1], scale=scale[:, 0:1]).then_inc(relu1, 1)
                act.wait_ge(relu1, i + 1)
                copy(h1_hi[:, i // 4, i % 4, 1:SH + 1, 1:SW + 1],
                     y[:, i, :].rearrange("p (r c) -> p r c", c=SW)).then_inc(h1_hi_done, 1)
            act.wait_ge(h1_lo_done, 8)
            for k in range(16):
                act.wait_ge(c2_done, k + 1)
                copy(y[:, k // 2, (k % 2) * HALF:(k % 2 + 1) * HALF], ps[:, k % 8, :]).then_inc(c2_copied, 1)
            root(2, BN2_ROOT)
            act.wait_ge(bn_dve, BN2_END)
            for i in range(8):
                if i == 0:
                    act.wait_ge(c2_copied, 16)
                act.activation(y[:, i, :], y[:, i, :], ACT.Relu, bias=shift[:, 1:2], scale=scale[:, 1:2]).then_inc(relu2, 1)
                act.wait_ge(relu2, i + 1)
                copy(h2_hi[:, i, :], y[:, i, :]).then_inc(h2_hi_done, 1)
            root(3, BN3_ROOT)
            act.wait_ge(bn_dve, BN3_END)
            for u in range(8):
                cb = u % 2
                for k in range(8):
                    h, a, b = k // 4, (k // 2) % 2, k % 2
                    act.wait_ge(f_added, 8 * u + k + 1)
                    if u >= 2 and k % 4 == 0:
                        act.wait_ge(out_stored[u % 2], 16 * (2 * (u // 2 - 1) + 2))
                    act.activation(outs[:, u % 2, 32 * h + a:32 * h + 32:2, b::2],
                                   x1in[:, u % 2, 2 * a + b, h * HALF:(h + 1) * HALF].rearrange("p (r c) -> p r c", c=SW),
                                   ACT.Relu, bias=shift[:, 2 + cb:3 + cb]).then_inc(f_out, 1)

        @block.tensor
        def _(pe):
            def mm3(dst, l_hi, l_lo, r_hi_, r_lo_, first, last, **kw):
                pe.matmul(dst, l_hi, r_hi_, start=first, stop=False, **kw)
                pe.matmul(dst, l_hi, r_lo_, start=False, stop=False, **kw)
                return pe.matmul(dst, l_lo, r_hi_, start=False, stop=last, **kw)

            pe.wait_ge(masked, 7)
            pe.wait_ge(small_loaded, 64)
            pe.transpose(psU[:, 0:KK], w2raw[:, :], ident[0:KK, 0:KK]).then_inc(prep_pe, 1)
            for kb in range(CB):
                pe.transpose(psT[:, kb * MID1:(kb + 1) * MID1], v1raw[:, kb * P:(kb + 1) * P],
                             ident[0:MID1, 0:MID1]).then_inc(prep_pe, 1)
            pe.wait_ge(prep_dve, 1)
            pe.matmul(psXT[0:KK, 0:1], w2T[:, :], b1s[:, :], start=True, stop=True).then_inc(prep_pe, 1)
            for i in range(CB * K):
                kb, v = i // K, i % K
                if v == 0:
                    pe.wait_ge(w1_loaded[kb], 16)
                if i >= 2:
                    pe.wait_ge(wlo_done, 2 + i - 1)
                for u in range(K):
                    mm = pe.matmul(psR[i % 2][:, u * KK:(u + 1) * KK], w1raw[:, kb, :, u * K + v], w2T[:, :],
                                   start=True, stop=True)
                mm.then_inc(weff_done, 1)
            pe.wait_ge(whi_done, 2 + CB * K)
            pe.wait_ge(wlo_done, 2 + CB * K)
            pe.wait_ge(sel_ready, 1)

            def step(n, q):
                s, p1, p2, p3 = (Step(n, q, d) for d in range(4))

                def conv(g, part):
                    h, m = g // 3, g % 3
                    rows = slice(HR * h, HR * h + HR)
                    dst = psR[g % 2][0:MS[m], :]
                    if part == 0:
                        if g == 0:
                            pe.wait_ge(xs_hi_done, s.count(2, 1))
                            pe.wait_ge(xs_lo_done, s.count(2, 1))
                        if g >= 2:
                            pe.wait_ge(r_lo_done, s.count(6, g - 2))
                        elif s.live(1):
                            pe.wait_ge(r_lo_done, p1.count(6, g + 4))
                    todo = [(kb, v) for kb in range(CB) for v in range(K)][7 * part:7 * part + 7]
                    for kb, v in todo:
                        cols = slice(v, v + SW)
                        mm = mm3(dst, w_hi[:, kb, v, MB * m:MB * m + MS[m]], w_lo[:, kb, v, MB * m:MB * m + MS[m]],
                                 xs_hi[:, s.b, kb, rows, cols], xs_lo[:, s.b, kb, rows, cols],
                                 (kb, v) == (0, 0), (kb, v) == (CB - 1, K - 1))
                    if part == 1:
                        mm.then_inc(group_done, 1)

                def usum(h):
                    if h == 0:
                        pe.wait_ge(r_hi_done, p1.count(6, 5))
                        pe.wait_ge(r_lo_done, p1.count(6, 5))
                        if p1.live(2):
                            pe.wait_ge(y1_done, p3.count(2, 0))
                    elif p1.live(1):
                        pe.wait_ge(attn_done, p2.count(2, 0))
                    bank = psU if h == 0 else psT
                    order = [PAD] + [u for u in range(K) if u != PAD]
                    parts = [(u, m) for u in order for m in range(3)
                             if KK * u < MB * m + MS[m] and KK * (u + 1) > MB * m]
                    for i, (u, m) in enumerate(parts):
                        lo, hi = max(HR * h, PAD - u), min(HR * h + HR, SH + PAD - u)
                        at = SELB - (MB * m - KK * u)
                        for j, r in enumerate((r_hi, r_lo)):
                            mm = pe.matmul(bank[0:KK, (lo - HR * h) * SW:(hi - HR * h) * SW], sel[0:MS[m], at:at + KK],
                                           r[0:MS[m], m, (lo + u - PAD) * SW:(hi + u - PAD) * SW],
                                           start=(i == 0 and j == 0), stop=(i == len(parts) - 1 and j == 1),
                                           skip_group_check=True)
                    mm.then_inc(usum_done, 1)

                def logits_T():
                    pe.wait_ge(logits_done, p1.count(2, 1))
                    pe.sem_inc(pe_gate, 1)
                    for t in range(NT):
                        mm = pe.transpose(psT[:, t * KK:(t + 1) * KK], logits[:, t * P:(t + 1) * P], ident[0:KK, 0:KK])
                    mm.then_inc(lt_done, 1)

                def attn_T(h):
                    bank = psT if h == 0 else psU
                    pe.wait_ge(probs_done, p1.count(1, 0))
                    if h == 1 and p3.live():
                        pe.wait_ge(y1_done, p3.count(2, 1))
                    pe.sem_inc(pe_gate, 1)
                    for t in range(4):
                        mm = pe.transpose(bank[0:KK, t * P:(t + 1) * P], probs[:, 4 * h + t, :], ident[:, :])
                    mm.then_inc(at_done, 1)

                def band_T(last):
                    if not last:
                        pe.wait_ge(attn_loaded, p2.dma(NT, NT - 1))
                        if p2.live(1):
                            pe.wait_ge(band_step, p3.count(NT * K, (NT - 1) * K - 1))
                        for t in range(NT - 1):
                            mm = pe.transpose(psB[:, t * JV:(t + 1) * JV], attn_jv[:, t, :], ident[0:JV, 0:JV])
                    else:
                        pe.wait_ge(xT_lo_done, p2.count(4, 2))
                        mm = pe.transpose(psXT[:, 0:JV], attn_jv[:, NT - 1, :], ident[0:JV, 0:JV])
                    mm.then_inc(bt_done, 1)

                def x_T(pair):
                    if pair % 2 == 0:
                        pe.wait_ge(xq_loaded[pair // 2], n * 64 + 32 * ((q - 2) // 2 + 1))
                    if pair == 3:
                        pe.wait_ge(band_step, p2.count(NT * K, NT * K - 1))
                    elif pair:
                        pe.wait_ge(xT_lo_done, p2.count(4, pair - 1))
                    elif p2.live(1):
                        pe.wait_ge(xT_lo_done, p3.count(4, 3))
                    for t in range(2):
                        r = 4 * (2 * pair + t)
                        for kb in range(CB):
                            mm = pe.transpose(psXT[:, t * C + kb * P:t * C + (kb + 1) * P],
                                              xq[:, kb, r:r + 4, p2.b::2], ident[:, :])
                    mm.then_inc(xt_done, 1)

                def unit(i):
                    h, t = UNITS[i]
                    first = t == TILES[h][0]
                    if first:
                        if h == 1:
                            pe.wait_ge(x1_lo_done, p2.count(4, 1))
                            pe.wait_ge(x1_done, p2.count(4, 1))
                        elif p2.live(1):
                            pe.wait_ge(x1_lo_done, p3.count(4, 3))
                            pe.wait_ge(x1_done, p3.count(4, 3))
                    pe.wait_ge(band_lo_done, p2.count(NT, t))
                    pe.wait_ge(xT_lo_done, p2.count(4, t // 2))
                    lo, hi = window(h, t)
                    win = slice(lo - (4 * t - PAD), hi - (4 * t - PAD))
                    for cb in range(CB):
                        cols = slice(cb * P, (cb + 1) * P)
                        mm = mm3(psX[cb][:, (lo - HR * h) * SW:(hi - HR * h) * SW],
                                 xT_hi[:, t % 4, cols], xT_lo[:, t % 4, cols],
                                 band_hi[:, t % 4, win, :], band_lo[:, t % 4, win, :],
                                 first, t == TILES[h][-1], skip_group_check=True)
                    mm.then_inc(unit_done, 1)

                def proj(p, h):
                    pe.wait_ge(x1_lo_done, p.count(4, 2 * h + 1))
                    if h == 1:
                        if Step(n, q, 1).live():
                            pe.wait_ge(logits_done, p1.count(2, 0))
                    elif p1.live():
                        pe.wait_ge(attn_done, p1.count(2, 1))
                    if h == 1 or p.live(1):
                        pe.wait_ge(y1_done, p.count(2, h) - 1)
                    for cb in range(CB):
                        for j, r in enumerate((x1_hi, x1_lo)):
                            mm = pe.matmul(psU, v1pack[:, cb, :], r[:, cb, h, :],
                                           start=(cb == 0 and j == 0), stop=(cb == CB - 1 and j == 1))
                    mm.then_inc(y_done, 1)

                main, two, one, three = main_live(n), p2.live(), p1.live(), p3.live()
                for slot in range(12):
                    if main:
                        conv(slot // 2, slot % 2)
                    if one and slot in (0, 1):
                        usum(slot)
                    if two and slot == 0:
                        band_T(False)
                    if two and slot in (0, 2, 4, 9):
                        x_T((0, 2, 4, 9).index(slot))
                    if one and slot == 2:
                        logits_T()
                    if three and slot == 3:
                        proj(p3, 1)
                    if one and slot in (4, 5):
                        attn_T(slot - 4)
                    if two and slot == 5:
                        band_T(True)
                    if two and 2 <= slot <= 6:
                        unit(slot - 2)
                    if two and 7 <= slot <= 11:
                        unit(slot - 2)
                    if two and slot == 8:
                        proj(p2, 0)

            each_step(pe, step)

            pe.wait_ge(bn_loaded, 16 * 16)
            pe.wait_ge(y1_done, 2 * STEPS)
            for t in range(9):
                if t == 8:
                    pe.wait_ge(v_lo_done, 2)
                pe.transpose(ps[:, t % 8, 0:MID1], v2raw[:, :, t::9], ident[0:MID1, 0:MID1]).then_inc(vt_done, 1)
            for cb in range(CB):
                pe.wait_ge(v_lo_done, 2 * (2 + cb))
                pe.transpose(ps[:, 1 + cb, 0:P], v3raw[:, cb, :, :], ident[:, :]).then_inc(vt_done, 1)

            def average(k, col):
                pe.wait_ge(bn_dve, k)
                pe.matmul(ps[:, 7, 0:1], gavg[:, :], mv[:, col:col + 1], start=True, stop=True).then_inc(bn_pe, 1)

            average(BN1_MEAN, 0)
            average(BN1_VAR, 4)
            pe.wait_ge(v_lo_done, 22)
            pe.wait_ge(v_hi_done, 22)
            pe.wait_ge(borders, 12)
            for k in range(16):
                sub, h = k // 2, k % 2
                n2, a, b = sub // 4, (sub // 2) % 2, sub % 2
                if k % 8 == 0:
                    pe.wait_ge(h1_lo_done, 4 * n2 + 4)
                if k >= 8:
                    pe.wait_ge(c2_copied, k - 7)
                for t in range(9):
                    ya, xb = a + t // 3 - 1, b + t % 3 - 1
                    r0, c0 = 1 + HR * h + ya // 2, 1 + xb // 2
                    src = slice(r0, r0 + HR), slice(c0, c0 + SW)
                    mm = mm3(ps[:, k % 8, :], v2_hi[:, t, :], v2_lo[:, t, :],
                             h1_hi[:, n2, (ya % 2) * 2 + xb % 2, src[0], src[1]],
                             h1_lo[:, n2, (ya % 2) * 2 + xb % 2, src[0], src[1]], t == 0, t == 8)
                mm.then_inc(c2_done, 1)
            average(BN2_MEAN, 0)
            average(BN2_VAR, 4)

            def last(k, cb, g, sub, h):
                return mm3(ps[:, k % 8, :], v3_hi[:, g, cb * P:(cb + 1) * P], v3_lo[:, g, cb * P:(cb + 1) * P],
                           h2_hi[:, sub, h * HALF:(h + 1) * HALF], h2_lo[:, sub, h * HALF:(h + 1) * HALF], True, True)

            for k in range(64):
                sub, g, h, cb = k // 8, (k // 4) % 2, (k // 2) % 2, k % 2
                if k % 8 == 0:
                    pe.wait_ge(h2_lo_done, sub + 1)
                if k >= 8:
                    pe.wait_ge(c3_stat, k - 7)
                last(k, cb, g, sub, h).then_inc(c3_done, 1)
            for k in range(64):
                u, h, a, b = k // 8, (k // 4) % 2, (k // 2) % 2, k % 2
                n2, g, cb = u // 4, (u // 2) % 2, u % 2
                if k < 8:
                    pe.wait_ge(c3_stat, 57 + k)
                else:
                    pe.wait_ge(f_added, k - 7)
                last(k, cb, g, 4 * n2 + 2 * a + b, h).then_inc(f_done, 1)

        @block.vector
        def _(dve):
            def minus(dst, a, b):
                return dve.tensor_tensor(dst, a, b, ALU.subtract)

            dve.wait_ge(prep_pe, 1)
            dve.tensor_copy(w2T[:, :], psU[:, 0:KK]).then_inc(prep_dve, 1)
            dve.wait_ge(whi_done, 2)
            for kb in range(CB):
                minus(v1pack[:, kb, MID1:P], psT[:, kb * MID1:(kb + 1) * MID1],
                      v1pack[:, kb, 0:MID1].bitcast(F32)).then_inc(wlo_done, 1)
            dve.wait_ge(prep_pe, 4)
            dve.wait_ge(small_loaded, 64)
            dve.tensor_tensor(beff[:, :], psXT[0:KK, 0:1], b2s[:, :], ALU.add).then_inc(prep_dve, 1)
            for i in range(CB * K):
                dve.wait_ge(whi_done, 3 + i)
                minus(w_lo[:, i // K, i % K, :], psR[i % 2][:, 0:UK], w_hi[:, i // K, i % K, :].bitcast(F32)
                      ).then_inc(wlo_done, 1)
            dve.wait_ge(masked, 7)
            dve.wait_ge(consts, 14)

            def step(n, q):
                s, p1, p2, p3 = (Step(n, q, d) for d in range(4))

                def x_out(p, h):
                    if p.live(1):
                        dve.wait_ge(y_done, p.ago(1).count(2, h))
                    for cb in range(CB):
                        dve.wait_ge(x1_done, p.count(4, 2 * h + cb))
                        minus(x1_lo[:, cb, h, :], psX[cb], x1_hi[:, cb, h, :].bitcast(F32)).then_inc(x1_lo_done, 1)

                def xT(pair):
                    slots = slice(2 * pair % 4, 2 * pair % 4 + 2)
                    dve.wait_ge(xT_hi_done, p2.count(4, pair))
                    wait_slot(dve, p2, 2 * pair + 1)
                    minus(xT_lo[:, slots, :], psXT.rearrange("p (t c) -> p t c", c=C), xT_hi[:, slots, :].bitcast(F32)
                          ).then_inc(xT_lo_done, 1)

                def build_band(t):
                    dve.wait_ge(bt_done, p2.count(2, t // (NT - 1)))
                    if t >= 2:
                        dve.wait_ge(band_lo_done, p2.count(NT, t - 2))
                    elif p2.live(1):
                        dve.wait_ge(band_lo_done, p3.count(NT, t + 6))
                    w = (psB[:, t * JV:(t + 1) * JV] if t < NT - 1 else psXT[:, 0:JV]).rearrange("p (j v) -> p j v", v=K)[:, ::-1, :]
                    for v in range(K):
                        if v or t or p2.live(1):
                            dve.wait_ge(band_step, p2.count(NT * K, t * K + v) - 1)
                        dve.sem_inc(dve_gate, 1)
                        dve.copy_predicated(band[:, t % 2, :, :],
                                            mask[:, v:v + 1, :].bitcast(U32).to_broadcast([P, WIN, SW]),
                                            w[:, :, v:v + 1].to_broadcast([P, WIN, SW])).then_inc(band_step, 1)

                def rlo(g):
                    h, m = g // 3, g % 3
                    part = slice(h * HALF, (h + 1) * HALF)
                    dve.wait_ge(r_hi_done, s.count(6, g))
                    minus(r_lo[0:MS[m], m, part], psR[g % 2][0:MS[m], :], r_hi[0:MS[m], m, part].bitcast(F32)
                          ).then_inc(r_lo_done, 1)

                def softmax_top():
                    dve.wait_ge(lt_done, p1.count(1, 0))
                    lt = psT[:, 0:NT * KK].rearrange("p (t k) -> p t k", k=KK)
                    dve.tensor_reduce(smx[:, 0, :], lt, AX_X, ALU.max).then_inc(max_done, 1)
                    dve.wait_ge(max_done, p1.count(1, 0))
                    if p1.live(1):
                        dve.wait_ge(probs_done, p2.count(1, 0))
                    minus(expo[:, :, :], lt, smx[:, 0, :].unsqueeze(2).to_broadcast([P, NT, KK])).then_inc(sub_done, 1)

                def softmax_end():
                    dve.wait_ge(exp_done, p1.count(1, 0))
                    dve.tensor_reduce(smx[:, 1, :], expo[:, :, :], AX_X, ALU.add).then_inc(norm_done, 1)
                    dve.wait_ge(norm_done, p1.count(2, 0))
                    dve.reciprocal(smx[:, 2, :], smx[:, 1, :]).then_inc(norm_done, 1)
                    dve.wait_ge(norm_done, p1.count(2, 1))
                    if p1.live(1):
                        dve.wait_ge(at_done, p2.count(2, 1))
                    dve.tensor_tensor(probs[:, :, :], expo[:, :, :],
                                      smx[:, 2, :].unsqueeze(2).to_broadcast([P, NT, KK]), ALU.mult
                                      ).then_inc(probs_done, 1)

                def y_out(p, h):
                    dve.wait_ge(yhalf_done, p.count(2, h))
                    if p.live(1):
                        dve.wait_ge(y1_stored, p.ago(1).dma(1, 0))
                    dve.tensor_tensor(y1[:, h, :], psU[0:MID1, :], y1half[:, :], ALU.add).then_inc(y1_done, 1)

                main, two, one, three = main_live(n), p2.live(), p1.live(), p3.live()
                if three:
                    x_out(p3, 1)
                if two:
                    xT(0), build_band(0), build_band(1)
                if main:
                    rlo(0)
                if two:
                    xT(1)
                if one:
                    softmax_top()
                if two:
                    build_band(2)
                if main:
                    rlo(1)
                if one:
                    softmax_end()
                if three:
                    y_out(p3, 1)
                if two:
                    build_band(3), xT(2), build_band(4)
                if main:
                    rlo(2)
                if two:
                    build_band(5)
                    x_out(p2, 0)
                    build_band(6)
                if main:
                    rlo(3)
                if two:
                    build_band(7), xT(3)
                    y_out(p2, 0)
                if main:
                    rlo(4)
                if main:
                    rlo(5)

            each_step(dve, step)

            dve.wait_ge(borders, 12)
            for t in range(9):
                for g in range(2):
                    rows = slice(64 * g, 64 * g + 64)
                    dve.wait_ge(v_hi_done, 2 * t + g + 1)
                    minus(v2_lo[rows, t, rows], ps[rows, t % 8, 0:MID1], v2_hi[rows, t, rows].bitcast(F32)
                          ).then_inc(v_lo_done, 1)
            for cb in range(CB):
                for g in range(2):
                    rows, cols = slice(64 * g, 64 * g + 64), slice(cb * P, (cb + 1) * P)
                    dve.wait_ge(v_hi_done, 18 + 2 * cb + g + 1)
                    minus(v3_lo[rows, g, cols], ps[rows, 1 + cb, 0:P], v3_hi[rows, g, cols].bitcast(F32)
                          ).then_inc(v_lo_done, 1)
            done = [0]

            def link(op):
                done[0] += 1
                op.then_inc(bn_dve, 1)
                dve.wait_ge(bn_dve, done[0])

            def affine(i, width, var, mean, gamma, beta, roots):
                link(dve.tensor_scalar(mv[:, 6:8], var, EPS, None, ALU.add))
                dve.wait_ge(bn_act, roots)
                sc, sh = scale[:, i:i + width], shift[:, i:i + width]
                link(dve.reciprocal(mv[:, 10:12], mv[:, 8:10]))
                link(dve.tensor_tensor(sc, mv[:, 10:10 + width], gamma, ALU.mult))
                link(dve.tensor_tensor(mv[:, 12:12 + width], mean, sc, ALU.mult))
                link(dve.tensor_tensor(sh, beta, mv[:, 12:12 + width], ALU.subtract))

            def norm(i, pes):
                link(dve.bn_aggr(mv[:, 0:2], stats[:, :, :].rearrange("p k e -> p (k e)")))
                dve.wait_ge(bn_pe, pes)
                link(dve.tensor_copy(mv[:, 2:3], ps[:, 7, 0:1]))
                link(dve.tensor_tensor(mv[:, 3:4], mv[:, 0:1], mv[:, 2:3], ALU.subtract))
                link(dve.scalar_tensor_tensor(out=mv[:, 4:5], in0=mv[:, 3:4], scalar=mv[:, 3:4], in1=mv[:, 1:2],
                                              op0=ALU.mult, op1=ALU.add))
                dve.wait_ge(bn_pe, pes + 1)
                link(dve.tensor_copy(mv[:, 5:6], ps[:, 7, 0:1]))
                affine(i, 1, mv[:, 5:6].to_broadcast([P, 2]), mv[:, 2:3], bn[:, 2 * i:2 * i + 1],
                       bn[:, 2 * i + 1:2 * i + 2], i + 1)

            dve.wait_ge(bn_loaded, 16 * 16)
            dve.wait_ge(y_loaded, 16 * 16)
            for k in range(16):
                dve.bn_stats(stats[:, k, :], y[:, k // 2, (k % 2) * HALF:(k % 2 + 1) * HALF]).then_inc(y_stat, 1)
            dve.wait_ge(y_stat, 16)
            norm(0, 1)
            for i in range(8):
                dve.wait_ge(h1_hi_done, i + 1)
                minus(h1_lo[:, i // 4, i % 4, 1:SH + 1, 1:SW + 1], y[:, i, :].rearrange("p (r c) -> p r c", c=SW),
                      h1_hi[:, i // 4, i % 4, 1:SH + 1, 1:SW + 1].bitcast(F32)).then_inc(h1_lo_done, 1)
            for k in range(16):
                dve.wait_ge(c2_copied, k + 1)
                dve.bn_stats(stats[:, k, :], y[:, k // 2, (k % 2) * HALF:(k % 2 + 1) * HALF]).then_inc(c2_stat, 1)
            dve.wait_ge(c2_stat, 16)
            norm(1, 3)
            for i in range(8):
                dve.wait_ge(h2_hi_done, i + 1)
                minus(h2_lo[:, i, :], y[:, i, :], h2_hi[:, i, :].bitcast(F32)).then_inc(h2_lo_done, 1)
            for k in range(64):
                dve.wait_ge(c3_done, k + 1)
                dve.bn_stats(stats3[:, k % 2, k // 2, :], ps[:, k % 8, :]).then_inc(c3_stat, 1)
            dve.wait_ge(c3_stat, 64)
            for cb in range(CB):
                link(dve.bn_aggr(mv[:, 2 * cb:2 * cb + 2], stats3[:, cb, :, :].rearrange("p k e -> p (k e)")))
            affine(2, 2, mv[:, 1:4:2], mv[:, 0:4:2], bn[:, 4:6], bn[:, 6:8], 3)
            for k in range(64):
                u, h, sub = k // 8, (k // 4) % 2, k % 4
                cb = u % 2
                if k % 8 == 0:
                    dve.wait_ge(x1_back[u % 2], 16 * (u // 2 + 1))
                dve.wait_ge(f_done, k + 1)
                part = x1in[:, u % 2, sub, h * HALF:(h + 1) * HALF]
                dve.scalar_tensor_tensor(out=part, in0=ps[:, k % 8, :], scalar=scale[:, 2 + cb:3 + cb], in1=part,
                                         op0=ALU.mult, op1=ALU.add).then_inc(f_added, 1)


BN1_MEAN, BN1_VAR, BN1_ROOT, BN1_END = 1, 4, 6, 10
BN2_MEAN, BN2_VAR, BN2_ROOT, BN2_END = 11, 14, 16, 20
BN3_ROOT, BN3_END = 23, 27

_INS = ["x", "L0_conv_w1", "L0_conv_b1", "L0_conv_w2", "L0_conv_b2", "L1_conv_w1", "L1_conv_g1", "L1_conv_b1",
        "L1_conv_w2", "L1_conv_g2", "L1_conv_b2", "L1_conv_w3", "L1_conv_g3", "L1_conv_b3"]


def kernel(**inputs):
    import concourse.bacc as bacc
    from concourse.bass_utils import run_bass_kernel_spmd

    nc = bacc.Bacc("TRN2", target_bir_lowering=False, num_devices=1, dynamic_dma_scratch_size=1024)
    arrays, args = {}, []
    for name in _INS:
        a = np.ascontiguousarray(inputs[name])
        arrays[f"in_{name}"] = a
        args.append(nc.dram_tensor(f"in_{name}", a.shape, mybir.dt.from_np(a.dtype), kind="ExternalInput").ap())
    args.append(nc.dram_tensor("out_0", (B, C, H, W), F32, kind="ExternalOutput").ap())
    build(nc, *args)
    r = run_bass_kernel_spmd(nc, [arrays], core_ids=[0])
    return r.results[0]["out_0"]
```

```python
from contextlib import ExitStack

import numpy as np

import concourse.bass as bass
from concourse import mybir

F32 = mybir.dt.float32
F32R = mybir.dt.float32r
U32 = mybir.dt.uint32
ALU = mybir.AluOpType
ACT = mybir.ActivationFunctionType
AX_X = mybir.AxisListType.X

P = 128
B, C, H, W = 4, 256, 64, 64
CB = C // P
K = 7
KK = K * K
MID0 = 128
SH, SW = H // 2, W // 2
SPX = SH * SW
HALF = SPX // 2
HR = SH // 2
PAD = K // 2
PW = SW + 2 * PAD
PH = SH + 2 * PAD
PLANE = PH * PW
UPLANES = K * (PLANE - 1) + PW
PLANES = (2 * K - 1) * UPLANES
UK = K * KK
MB = 115
MS = [MB, MB, UK - 2 * MB]
NT = SH // 4
WIN = 4 + 2 * PAD
JV = WIN * K
MID1 = 64
STEPS = 4 * B
EPS = 1e-5
SELB = KK
SELW = SELB + MB + KK
LAG = 3


def window(h, t):
    return max(4 * t - PAD, HR * h), min(4 * t + 4 + PAD, HR * h + HR)


MIDDLE, EVEN, ODD = 0, 1, 2
TAPS = {MIDDLE: (K + 1) // 2, EVEN: (K + 1) // 2, ODD: K // 2}
SIGW = {MIDDLE: SW // 2 + 3, EVEN: SW // 2 + 3, ODD: SW // 2 + 2}
GROUPS = [(prod, m) for prod in (MIDDLE, EVEN, ODD) for m in range(3)]
TRIPLES = [(g, cb, j) for g, (prod, m) in enumerate(GROUPS) for cb in range(CB) for j in range(TAPS[prod])]
NG = len(GROUPS)
NW = 10


def weight_of(prod, j):
    if prod == MIDDLE and j < K // 2:
        return 7 + j
    return 4 + j if prod == ODD else j


TILES = [[t for t in range(NT) if window(h, t)[0] < window(h, t)[1]] for h in range(2)]
UNITS = [(h, t) for h in range(2) for t in TILES[h]]


def build(nc, x, w1, b1, w2, b2, v1, g1, c1, v2, g2, c2, v3, g3, c3, out):
    attn_planes = nc.dram_tensor("attn_planes", (2, PLANES), F32, kind="Internal").ap()
    x1_dram = nc.dram_tensor("x1_dram", (STEPS, CB, P, SPX), F32, kind="Internal").ap()
    y1_dram = nc.dram_tensor("y1_dram", (STEPS, MID1, SPX), F32, kind="Internal").ap()

    top = ExitStack()
    with top:
        def sem(name):
            return top.enter_context(nc.semaphore(name))

        def sb(stack, name, shape, dt=F32):
            return stack.enter_context(nc.sbuf_tensor(name, shape, dt))

        ps = top.enter_context(nc.psum_tensor("ps", [P, 8, 512], F32))
        psR = [ps[:, 0, :], ps[:, 1, :]]
        psX = [ps[:, 2, :], ps[:, 3, :]]
        psU, psT, psXT, psB = ps[:, 4, :], ps[:, 5, :], ps[:, 6, :], ps[:, 7, :]

        ident = sb(top, "ident", [P, P])
        gavg = sb(top, "gavg", [P, P])
        stats1 = sb(top, "stats1", [MID1, 2 * STEPS, 6])
        bn = sb(top, "bn", [P, 8])

        l0 = ExitStack()
        w_hi = sb(l0, "w_hi", [P, CB, NW, UK], F32R)
        w_lo = sb(l0, "w_lo", [P, CB, NW, UK], F32R)
        xraw = sb(l0, "xraw", [P, CB, SH, W + 4 * PAD])
        mid_hi = sb(l0, "mid_hi", [P, CB, SH, SIGW[MIDDLE]], F32R)
        mid_lo = sb(l0, "mid_lo", [P, CB, SH, SIGW[MIDDLE]], F32R)
        even_hi = sb(l0, "even_hi", [P, CB, SH, SIGW[EVEN]], F32R)
        even_lo = sb(l0, "even_lo", [P, CB, SH, SIGW[EVEN]], F32R)
        odd_hi = sb(l0, "odd_hi", [P, 2, CB, SH, SIGW[ODD]], F32R)
        odd_lo = sb(l0, "odd_lo", [P, 2, CB, SH, SIGW[ODD]], F32R)
        diff = sb(l0, "diff", [P, SH, SIGW[EVEN]])
        middle = sb(l0, "middle", [P, 3, HALF])
        evens = sb(l0, "evens", [P, HALF])
        r_hi = sb(l0, "r_hi", [P, 3, SPX], F32R)
        r_lo = sb(l0, "r_lo", [P, 3, SPX], F32R)
        l0r = ExitStack()
        sel = sb(l0r, "sel", [P, SELW], F32R)
        mask = sb(l0r, "mask", [P, K, SW])
        v1pack = sb(l0r, "v1pack", [P, CB, P], F32R)
        band = sb(l0r, "band", [P, 2, WIN, SW])
        beff = sb(l0r, "beff", [KK, 1])
        w2T = sb(l0r, "w2T", [P, KK])
        b1s = sb(l0r, "b1s", [P, 1])
        b2s = sb(l0r, "b2s", [KK, 1])
        l0a = ExitStack()
        w1raw = sb(l0a, "w1raw", [P, CB, P, KK])
        w2raw = sb(l0a, "w2raw", [KK, P])
        v1raw = sb(l0a, "v1raw", [MID1, C])
        zeros = sb(l0a, "zeros", [P, 1024])
        self32 = sb(l0a, "self32", [P, SELW])
        wtmp = sb(l0a, "wtmp", [P, UK])
        wsum = sb(l0a, "wsum", [P, UK])
        l0a.close()
        l0b = ExitStack()
        logits = sb(l0b, "logits", [KK, SPX])
        attn = sb(l0b, "attn", [KK, SPX])
        probs = sb(l0b, "probs", [P, NT, KK])
        smx = sb(l0b, "smx", [P, 3, NT])
        attn_jv = sb(l0b, "attn_jv", [JV, NT, P])
        xq = sb(l0b, "xq", [P, CB, SH, W])
        xT_hi = sb(l0b, "xT_hi", [P, 4, C], F32R)
        xT_lo = sb(l0b, "xT_lo", [P, 4, C], F32R)
        band_hi = sb(l0b, "band_hi", [P, 4, WIN, SW], F32R)
        band_lo = sb(l0b, "band_lo", [P, 4, WIN, SW], F32R)
        x1 = sb(l0b, "x1", [P, CB, HALF])
        x1_hi = sb(l0b, "x1_hi", [P, CB, HALF], F32R)
        x1_lo = sb(l0b, "x1_lo", [P, CB, HALF], F32R)
        y1 = sb(l0b, "y1", [MID1, 2, HALF])
        l0b.close()
        l0r.close()
        l0.close()

        l1 = ExitStack()
        y = sb(l1, "y", [P, 8, SPX])
        v2_hi = sb(l1, "v2_hi", [P, 9, P], F32R)
        v2_lo = sb(l1, "v2_lo", [P, 9, P], F32R)
        v3_hi = sb(l1, "v3_hi", [P, 2, C], F32R)
        v3_lo = sb(l1, "v3_lo", [P, 2, C], F32R)
        v3raw = sb(l1, "v3raw", [P, CB, 2, MID1])
        v2raw = sb(l1, "v2raw", [MID1, 2, MID1 * 9])
        l1a = ExitStack()
        h1_hi = sb(l1a, "h1_hi", [P, 2, 4, SH + 2, SW + 2], F32R)
        h1_lo = sb(l1a, "h1_lo", [P, 2, 4, SH + 2, SW + 2], F32R)
        l1a.close()
        l1b = ExitStack()
        x1in = sb(l1b, "x1in", [P, 4, 4, SPX])
        spare = sb(l1b, "spare", [P, 2 * 8 * (SH + 2) * (SW + 2) - 16 * SPX])
        h2_hi = sb(l1b, "h2_hi", [P, 8, SPX], F32R)
        h2_lo = sb(l1b, "h2_lo", [P, 8, SPX], F32R)
        stats = sb(l1b, "stats", [P, 16, 6])
        stats3 = sb(l1b, "stats3", [P, CB, 32, 6])
        mv = sb(l1b, "mv", [P, 16])
        scale = sb(l1b, "scale", [P, 4])
        shift = sb(l1b, "shift", [P, 4])
        l1b.close()
        l1.close()
        outs = [y[:, 4 * k:4 * k + 4, :].rearrange("p i e -> p (i e)").rearrange("p (r c) -> p r c", c=W) for k in range(2)]

        zeroed, consts, masked, sel_ready = sem("zeroed"), sem("consts"), sem("masked"), sem("sel_ready")
        small_loaded, bn_loaded, w1_loaded = sem("small_loaded"), sem("bn_loaded"), [sem("w1_loaded0"), sem("w1_loaded1")]
        planes_zero = sem("planes_zero")
        prep_pe, prep_dve = sem("prep_pe"), sem("prep_dve")
        weff_done, whi_done, wlo_done = sem("weff_done"), sem("whi_done"), sem("wlo_done")
        v1_hi_done, v1_lo_done = sem("v1_hi_done"), sem("v1_lo_done")
        wcopy_done, wsum_done, wsum_hi_done, wsum_lo_done = sem("wcopy_done"), sem("wsum_done"), sem("wsum_hi_done"), sem("wsum_lo_done")
        x_loaded, diff_done, sig_hi_done, sig_lo_done = sem("x_loaded"), sem("diff_done"), sem("sig_hi_done"), sem("sig_lo_done")
        group_done, middle_done, outputs_done = sem("group_done"), sem("middle_done"), sem("outputs_done")
        r_hi_done, r_lo_done = sem("r_hi_done"), sem("r_lo_done")
        usum_done, logits_done, lt_done = sem("usum_done"), sem("logits_done"), sem("lt_done")
        max_done, sub_done, exp_done = sem("max_done"), sem("sub_done"), sem("exp_done")
        norm_done, probs_done = sem("norm_done"), sem("probs_done")
        at_done, attn_done, attn_stored, attn_loaded = sem("at_done"), sem("attn_done"), sem("attn_stored"), sem("attn_loaded")
        bt_done, band_step, band_hi_done, band_lo_done = sem("bt_done"), sem("band_step"), sem("band_hi_done"), sem("band_lo_done")
        xq_loaded = [sem("xq_loaded0"), sem("xq_loaded1")]
        xt_done, xT_hi_done, xT_lo_done = sem("xt_done"), sem("xT_hi_done"), sem("xT_lo_done")
        unit_done, x1_hi_done, x1_done, x1_lo_done = sem("unit_done"), sem("x1_hi_done"), sem("x1_done"), sem("x1_lo_done")
        y_done, yhalf_done, y1_done = sem("y_done"), sem("yhalf_done"), sem("y1_done")
        y1_stat = sem("y1_stat")
        x1_stored, y1_stored = [sem("x1_stored0"), sem("x1_stored1")], sem("y1_stored")
        v_loaded = sem("v_loaded")
        y_loaded, borders, corners, vt_done, v_hi_done, v_lo_done = [sem("y_loaded0"), sem("y_loaded1")], sem("borders"), sem("corners"), sem("vt_done"), sem("v_hi_done"), sem("v_lo_done")
        dve_gate, pe_gate, sp_gate = sem("dve_gate"), sem("pe_gate"), sem("sp_gate")
        bn_dve, bn_pe, bn_act = sem("bn_dve"), sem("bn_pe"), sem("bn_act")
        relu1, h1_hi_done, h1_lo_done = sem("relu1"), sem("h1_hi_done"), sem("h1_lo_done")
        relu2, h2_hi_done, h2_lo_done = sem("relu2"), sem("h2_hi_done"), sem("h2_lo_done")
        c2_done, c2_copied, c2_stat = sem("c2_done"), sem("c2_copied"), sem("c2_stat")
        c3_done, c3_stat = sem("c3_done"), sem("c3_stat")
        f_done, f_added, f_out = sem("f_done"), sem("f_added"), sem("f_out")
        x1_back = [sem(f"x1_back{k}") for k in range(4)]
        out_stored = [sem("out_stored0"), sem("out_stored1")]

        class Step:

            def __init__(self, n, q, back=0):
                self.n, self.q, self.back = n, q, back
                self.k = q - back
                self.b = self.k % 2
                self.a = (self.k // 2) % 2

            def live(self, ago=0):
                return not isinstance(self.n, int) or 0 <= 4 * self.n + self.k - ago < STEPS

            def count(self, per_step, i):
                return self.n * (4 * per_step) + (self.k * per_step + i + 1)

            def dma(self, per_step, i):
                return self.n * (64 * per_step) + 16 * (self.k * per_step + i + 1)

            def index(self):
                return self.n * 4 + self.k

            def image(self):
                return self.n + self.k // 4

            def ago(self, m):
                return Step(self.n, self.q, self.back + m)

        def each_step(eng, step, prepare=None):
            for q in range(4):
                step(0, q)
            with eng.Fori(1, B) as n:
                for q in range(4):
                    step(n, q)
            for q in range(LAG):
                step(B, q)
                if q == 0 and prepare:
                    prepare()

        def main_live(n):
            return not isinstance(n, int) or n < B

        block = top.enter_context(nc.Block())

        def store_out(sp, u):
            n2, g, cb = u // 4, (u // 2) % 2, u % 2
            for h in range(2):
                sp.wait_ge(f_out, 8 * u + 4 * h + 4)
                sp.dma_start(out[2 * g + n2, cb * P:(cb + 1) * P, 32 * h:32 * h + 32, :],
                             outs[u % 2][:, 32 * h:32 * h + 32, :]).then_inc(out_stored[u % 2], 16)

        def load_rows(sp, dst, n, a, done, r0=0, r1=SH):
            for cb in range(CB):
                src = x[n, cb * P:(cb + 1) * P].rearrange("p (r a) w -> p r a w", a=2)[:, r0:r1, a, :]
                sp.dma_start(dst[:, cb, r0:r1, :], src).then_inc(done, 16)

        def signal(s, piece, cb):
            if piece == 1:
                return mid_hi[:, cb, :, :], mid_lo[:, cb, :, :], phase(s, cb, 1, SIGW[MIDDLE])
            if piece == 0:
                return odd_hi[:, s.b, cb, :, :], odd_lo[:, s.b, cb, :, :], diff[:, :, 0:SIGW[ODD]]
            return even_hi[:, cb, :, :], even_lo[:, cb, :, :], diff[:, :, 0:SIGW[EVEN]]

        def phase(s, cb, k, width):
            first = 2 * k + s.b
            return xraw[:, cb, :, first:first + 4 * width - 3:4]

        def r_part(r, m, e):
            return r[0:MS[m], m, :].rearrange("p (r c e) -> p e r c", c=SW // 2, e=2)[:, e]

        def filtered(m, e):
            t = evens[0:MS[m], :] if e == 0 else middle[0:MS[m], m, :]
            return t.rearrange("p (r c) -> p r c", c=SW // 2)

        def v2_of(rows, k):
            n = 5 - k
            return psR[k][rows, 0:n * MID1].rearrange("p (t m) -> p t m", m=MID1)

        def last_unit(t):
            return max(i for i, (h, tt) in enumerate(UNITS) if tt == t)

        def wait_slot(eng, p, t):
            if t >= 4:
                eng.wait_ge(unit_done, p.count(len(UNITS), last_unit(t - 4)))
            elif p.live(1):
                eng.wait_ge(unit_done, p.ago(1).count(len(UNITS), last_unit(t + 4)))

        @block.sync
        def _(sp):
            sp.dma_start(w2raw[:, :], w2.rearrange("k o a b -> k (o a b)")).then_inc(small_loaded, 16)
            sp.dma_start(v1raw[:, :], v1.rearrange("m c a b -> m (c a b)")).then_inc(small_loaded, 16)
            sp.dma_start(b1s[:, :], b1.rearrange("(p a) -> p a", a=1)).then_inc(small_loaded, 16)
            sp.dma_start(b2s[:, :], b2.rearrange("(p a) -> p a", a=1)).then_inc(small_loaded, 16)
            for kb in range(CB):
                sp.dma_start(w1raw[:, kb, :, :].rearrange("p c t -> p (c t)"),
                             w1[:, kb * P:(kb + 1) * P, :, :].rearrange("o c u v -> o (c u v)")
                             ).then_inc(w1_loaded[kb], 16)
                if kb == 0:
                    load_rows(sp, xraw[:, :, :, 2 * PAD:2 * PAD + W], 0, 0, x_loaded)
            sp.wait_ge(zeroed, 1)
            total = 2 * PLANES
            flat = attn_planes.rearrange("s e -> (s e)")
            whole = total // (P * 1024)
            for i in range(whole):
                sp.dma_start(flat[i * P * 1024:(i + 1) * P * 1024].rearrange("(p e) -> p e", p=P),
                             zeros[:, :]).then_inc(planes_zero, 16)
            rest = total - whole * P * 1024
            rows = rest // 1024
            sp.dma_start(flat[whole * P * 1024:(whole * P + rows) * 1024].rearrange("(p e) -> p e", p=rows),
                         zeros[0:rows, :]).then_inc(planes_zero, 16)
            tail = rest - rows * 1024
            if tail:
                sp.dma_start(flat[total - tail:total].rearrange("(p e) -> p e", p=1),
                             zeros[0:1, 0:tail]).then_inc(planes_zero, 16)
            for g in range(2):
                for i, t in enumerate((g1, c1, g2, c2)):
                    sp.dma_start(bn[64 * g:64 * g + 64, i:i + 1], t.rearrange("(p a) -> p a", a=1)).then_inc(bn_loaded, 16)
            for i, t in enumerate((g3, c3)):
                for cb in range(CB):
                    sp.dma_start(bn[:, 4 + 2 * i + cb:5 + 2 * i + cb],
                                 t[cb * P:(cb + 1) * P].rearrange("(p a) -> p a", a=1)).then_inc(bn_loaded, 16)
            sp.wait_ge(planes_zero, 16 * (whole + 1 + bool(tail)))

            def step(n, q):
                s, p1, p2, p3 = (Step(n, q, d) for d in range(4))
                at3, at2, following = p3.index(), p2.index(), (n + 1) % B
                if not isinstance(n, int):
                    at3, at2 = sp.snap(at3), sp.snap(at2)
                    following = sp.snap(following) if q == 2 else None
                if p3.live():
                    sp.wait_ge(x1_done, p3.count(4, 3))
                    store_x1(at3, 1)
                if p3.live():
                    sp.wait_ge(y1_done, p3.count(2, 1))
                    sp.dma_start(y1_dram[at3], y1[:, :, :].rearrange("m h e -> m (h e)")).then_inc(y1_stored, 16)
                if p1.live():
                    sp.wait_ge(attn_done, p1.count(2, 1))
                    sp.sem_inc(sp_gate, 1)
                    if p1.live(2):
                        sp.wait_ge(attn_loaded, p1.ago(2).dma(NT, NT - 1))
                    for u in range(K):
                        sp.dma_start(bass.AP(tensor=attn_planes.tensor,
                                             offset=p1.b * PLANES + (PAD + u) * UPLANES + PAD * PW + PAD,
                                             ap=[[PLANE, K], [PW, SH], [1, SW]]),
                                     attn[u * K:(u + 1) * K, :].rearrange("k (r c) -> k r c", c=SW)).then_inc(attn_stored, 16)
                if p2.live():
                    sp.wait_ge(x1_done, p2.count(4, 1))
                    store_x1(at2, 0)
                if q % 2 == 1 and main_live(n):
                    load_xq(n, s, p2, 0)
                if p1.live():
                    sp.wait_ge(attn_stored, p1.dma(K, K - 1))
                    sp.sem_inc(sp_gate, 1)
                    if p1.live(1):
                        sp.wait_ge(bt_done, p2.count(2, 1))
                    for t in range(NT):
                        src = bass.AP(tensor=attn_planes.tensor,
                                      offset=p1.b * PLANES + (4 * t + WIN - 1) * PW + 2 * PAD,
                                      ap=[[PLANE - 1, JV], [UPLANES, 4], [1, SW]])
                        sp.dma_start(attn_jv[:, t, :], src).then_inc(attn_loaded, 16)
                if q % 2 == 0 and main_live(n):
                    sp.wait_ge(sig_lo_done, s.ago(-1).count(6, 5))
                    sp.sem_inc(sp_gate, 1)
                    load_rows(sp, xraw[:, :, :, 2 * PAD:2 * PAD + W], n if q == 0 else following, 1 if q == 0 else 0,
                              x_loaded)
                if q % 2 == 1 and main_live(n):
                    load_xq(n, s, p2, 1)

            def store_x1(at, h):
                sp.dma_start(x1_dram[at][:, :, h * HALF:(h + 1) * HALF].rearrange("b p e -> p b e"),
                             x1[:, :, :]).then_inc(x1_stored[h], 16)

            def load_xq(n, s, p2, half):
                if p2.live():
                    sp.wait_ge(xt_done, p2.count(4, 1 if half == 0 else 3))
                    sp.sem_inc(sp_gate, 1)
                else:
                    sp.wait_ge(group_done, 1)
                load_rows(sp, xq, n, s.a, xq_loaded[half], half * HR, half * HR + HR)

            def prepare():
                sp.wait_ge(group_done, NG * STEPS)
                sp.wait_ge(usum_done, 2 * STEPS)
                sp.wait_ge(r_lo_done, 6 * STEPS)
                sp.wait_ge(sig_lo_done, 6 * (STEPS + 1))
                for g in range(2):
                    sp.dma_start(v3raw[:, :, g, :], v3.rearrange("(b p) m x y -> p b (m x y)", p=P)).then_inc(v_loaded, 16)
                    sp.dma_start(v2raw[:, g, :], v2.rearrange("o i y x -> o (i y x)")).then_inc(v_loaded, 16)
                for i in range(8):
                    load_y(i, 0)
                for i in range(STEPS - LAG - 8 + 1):
                    load_y(i, 1)

            def load_y(i, g):
                sp.wait_ge(y1_stored, 16 * (8 * g + i + 1))
                sp.dma_start(y[64 * g:64 * g + 64, i, :], y1_dram[8 * g + i]).then_inc(y_loaded[g], 16)

            each_step(sp, step, prepare)

            for i in range(STEPS - LAG - 8 + 1, 8):
                load_y(i, 1)
            for h in range(2):
                sp.wait_ge(x1_stored[h], 16 * STEPS)
            sp.wait_ge(c2_done, 16)
            for u in range(8 + 3):
                if u < 8:
                    n2, g, cb = u // 4, (u // 2) % 2, u % 2
                    if u >= 4:
                        sp.wait_ge(f_out, 8 * (u - 3))
                    s0 = 8 * g + 4 * n2
                    sp.dma_start(x1in[:, u % 4, :, :], x1_dram[s0:s0 + 4, cb].rearrange("s p e -> p s e")
                                 ).then_inc(x1_back[u % 4], 16)
                if u >= 3:
                    store_out(sp, u - 3)
            for k in range(2):
                sp.wait_ge(out_stored[k], 16 * 8)

        @block.gpsimd
        def _(pool):
            pool.memset(zeros[:, :], 0.0).then_inc(zeroed, 1)
            for t in (ident[:, :], gavg[:, :], self32[:, :], mask[:, :, :]):
                pool.memset(t, 0.0).then_inc(consts, 1)
            for c0 in (0, 2 * PAD + W):
                pool.memset(xraw[:, :, :, c0:c0 + 2 * PAD], 0.0).then_inc(consts, 1)
            pool.memset(band[:, :, :, :], 0.0).then_inc(consts, 1)
            pool.wait_ge(consts, 7)

            puts = [(ident[:, :], 1.0, 0, [[-1, P]], 1), (gavg[:, :], 0.5, 0, [[-1, P]], 1),
                    (self32[:, :], 1.0, -SELB, [[1, SELW]], -1)]
            puts += [(mask[32 * g:32 * g + 32, :, :], 1.0, -PAD, [[1, K], [1, SW]], -1) for g in range(4)]
            puts += [(gavg[:, :], 0.5, d, [[-1, P]], 1) for d in (64, -64)]
            for i, (t, value, base, pattern, per_partition) in enumerate(puts):
                if i:
                    pool.wait_ge(masked, i)
                pool.affine_select(out=t, in_=t, compare_op=ALU.not_equal, fill=value, base=base, pattern=pattern,
                                   channel_multiplier=per_partition).then_inc(masked, 1)
            pool.wait_ge(masked, len(puts))

            def sig_lo(s, piece, cb):
                pool.wait_ge(sig_hi_done, s.count(6, 2 * piece + cb))
                hi, lo, src = signal(s, piece, cb)
                pool.tensor_tensor(lo, src, hi.bitcast(F32), ALU.subtract).then_inc(sig_lo_done, 1)

            for i in range(6):
                sig_lo(Step(0, 0), i // 2, i % 2)

            def step(n, q):
                s, p1, p2, p3 = (Step(n, q, d) for d in range(4))
                nxt = Step(n, q, -1)

                def band_tile(t):
                    pool.wait_ge(band_hi_done, p2.count(NT, t))
                    wait_slot(pool, p2, t)
                    pool.tensor_tensor(band_lo[:, t % 4, :, :], band[:, t % 2, :, :],
                                       band_hi[:, t % 4, :, :].bitcast(F32), ALU.subtract
                                       ).then_inc(band_lo_done, 1)

                def rlo(e, m):
                    i = 3 * e + m
                    pool.wait_ge(r_hi_done, s.count(6, i))
                    pool.tensor_tensor(r_part(r_lo, m, e), filtered(m, e), r_part(r_hi, m, e).bitcast(F32),
                                       ALU.subtract).then_inc(r_lo_done, 1)

                main, two = main_live(n), p2.live()
                if two:
                    band_tile(0)
                if main:
                    sig_lo(nxt, 0, 0)
                    sig_lo(nxt, 0, 1)
                if two:
                    band_tile(1)
                    band_tile(2)
                    band_tile(3)
                    band_tile(4)
                if main:
                    sig_lo(nxt, 1, 0)
                    rlo(0, 0)
                    sig_lo(nxt, 1, 1)
                if two:
                    band_tile(5)
                if main:
                    rlo(0, 1)
                if two:
                    band_tile(6)
                if main:
                    sig_lo(nxt, 2, 0)
                if two:
                    band_tile(7)
                if main:
                    rlo(0, 2)
                    sig_lo(nxt, 2, 1)
                    rlo(1, 0)
                    rlo(1, 1)
                    rlo(1, 2)

            def prepare():
                pool.wait_ge(group_done, NG * STEPS)
                pool.wait_ge(usum_done, 2 * STEPS)
                pool.wait_ge(sig_lo_done, 6 * (STEPS + 1))
                for t in (v2_hi, v2_lo, v3_hi, v3_lo):
                    pool.memset(t[:, :, :].bitcast(F32), 0.0).then_inc(corners, 1)
                for t in (h1_hi, h1_lo):
                    for e in (0, SH + 1):
                        pool.memset(t[:, :, :, e, :].bitcast(F32), 0.0).then_inc(borders, 1)
                        pool.memset(t[:, :, :, 1:SH + 1, e:e + 1].bitcast(F32), 0.0).then_inc(borders, 1)

            each_step(pool, step, prepare)

        @block.scalar
        def _(act):
            def copy(dst, src):
                return act.activation(dst, src, ACT.Copy)

            act.wait_ge(prep_pe, 3)
            for kb in range(CB):
                copy(v1pack[:, kb, 0:MID1], psT[:, kb * MID1:(kb + 1) * MID1]).then_inc(v1_hi_done, 1)
            act.wait_ge(masked, 7)
            copy(sel[:, :], self32[:, :]).then_inc(sel_ready, 1)
            act.wait_ge(consts, 7)

            def sig_hi(s, piece, cb):
                if piece != 1:
                    act.wait_ge(diff_done, s.count(4, piece + cb))
                if piece and cb == 0 and s.back:
                    act.wait_ge(group_done, s.ago(1).count(NG, 3 * piece - 1))
                hi, lo, src = signal(s, piece, cb)
                copy(hi, src).then_inc(sig_hi_done, 1)

            act.wait_ge(x_loaded, 32)
            for i in range(6):
                sig_hi(Step(0, 0), i // 2, i % 2)
            for i in range(CB * K):
                cb, v = i // K, i % K
                act.wait_ge(weff_done, i + 1)
                copy(w_hi[:, cb, v // 2 + 4 * (v % 2), :], psR[i % 2][:, 0:UK]).then_inc(whi_done, 1)
                k = 3 * cb + v // 2
                if v % 2 == 0 and v < K - 1:
                    if k:
                        act.wait_ge(wsum_done, k)
                    copy(wtmp[:, :], psR[i % 2][:, 0:UK]).then_inc(wcopy_done, 1)
                if v % 2 == 1:
                    act.wait_ge(wsum_done, k + 1)
                    copy(w_hi[:, cb, 7 + v // 2, :], wsum[:, :]).then_inc(wsum_hi_done, 1)

            def step(n, q):
                s, p1, p2, p3 = (Step(n, q, d) for d in range(4))
                nxt = Step(n, q, -1)

                def x_out(p, h):
                    act.wait_ge(unit_done, p.count(len(UNITS), 4 if h == 0 else 9))
                    if h == 1:
                        act.wait_ge(y_done, p.count(2, 0))
                    elif p.live(1):
                        act.wait_ge(y_done, p.ago(1).count(2, 1))
                    for cb in range(CB):
                        copy(x1_hi[:, cb, :], psX[cb]).then_inc(x1_hi_done, 1)
                    if h == 1:
                        act.wait_ge(x1_stored[0], p.dma(1, 0))
                    elif p.live(1):
                        act.wait_ge(x1_stored[1], p.ago(1).dma(1, 0))
                    for cb in range(CB):
                        copy(x1[:, cb, :], psX[cb]).then_inc(x1_done, 1)

                def logit(h):
                    act.wait_ge(usum_done, p1.count(2, h))
                    if p1.live(1) and h == 0:
                        act.wait_ge(lt_done, p2.count(1, 0))
                    act.activation(logits[:, h * HALF:(h + 1) * HALF], (psU if h == 0 else psT)[0:KK, :],
                                   ACT.Identity, bias=beff[:, 0:1]).then_inc(logits_done, 1)

                def xT(pair):
                    t = 2 * pair
                    act.wait_ge(xt_done, p2.count(4, pair))
                    wait_slot(act, p2, t + 1)
                    copy(xT_hi[:, t % 4:t % 4 + 2, :], psXT.rearrange("p (t c) -> p t c", c=C)).then_inc(xT_hi_done, 1)

                def bandhi(t):
                    act.wait_ge(band_step, p2.count(NT * K, t * K + K - 1))
                    wait_slot(act, p2, t)
                    copy(band_hi[:, t % 4, :, :], band[:, t % 2, :, :]).then_inc(band_hi_done, 1)

                def mid(m):
                    act.wait_ge(group_done, s.count(NG, m))
                    copy(middle[0:MS[m], m, :], psR[(m + s.b) % 2][0:MS[m], :]).then_inc(middle_done, 1)

                def rhi(e, m):
                    act.wait_ge(outputs_done, s.count(6, 3 * e + m))
                    if p1.live() and e == 0 and m == 0:
                        act.wait_ge(usum_done, p1.count(2, 1))
                    copy(r_part(r_hi, m, e), filtered(m, e)).then_inc(r_hi_done, 1)

                def attn_out(h):
                    act.wait_ge(at_done, p1.count(2, h))
                    if h == 0 and p1.live(1):
                        act.wait_ge(attn_stored, p2.dma(K, K - 1))
                    copy(attn[:, h * HALF:(h + 1) * HALF], (psT if h == 0 else psU)[0:KK, :]).then_inc(attn_done, 1)

                def yhalf(p, h):
                    act.wait_ge(y_done, p.count(2, h))
                    if p.live(1):
                        act.wait_ge(y1_stored, p.ago(1).dma(1, 0))
                    copy(y1[:, h, :], psU[MID1:P, :]).then_inc(yhalf_done, 1)

                def exponentials():
                    act.wait_ge(sub_done, p1.count(1, 0))
                    act.activation(probs[:, :, :], probs[:, :, :], ACT.Exp).then_inc(exp_done, 1)

                main, two, one, three = main_live(n), p2.live(), p1.live(), p3.live()
                if three:
                    x_out(p3, 1)
                if two:
                    xT(0)
                if one:
                    logit(0)
                if two:
                    bandhi(0)
                if one:
                    logit(1)
                if two:
                    bandhi(1)
                if main:
                    sig_hi(nxt, 0, 0)
                    mid(0)
                    mid(1)
                    sig_hi(nxt, 0, 1)
                if two:
                    xT(1)
                if main:
                    if q % 2 == 1:
                        act.wait_ge(x_loaded, n * 64 + 32 * ((q + 1) // 2 + 1))
                    sig_hi(nxt, 1, 0)
                if one:
                    exponentials()
                if two:
                    bandhi(2)
                if three:
                    yhalf(p3, 1)
                if main:
                    sig_hi(nxt, 1, 1)
                    mid(2)
                if two:
                    xT(2)
                    bandhi(3)
                    bandhi(4)
                if one:
                    attn_out(0)
                    attn_out(1)
                if main:
                    rhi(0, 0)
                    rhi(0, 1)
                if two:
                    bandhi(5)
                    x_out(p2, 0)
                    bandhi(6)
                if main:
                    sig_hi(nxt, 2, 0)
                    rhi(0, 2)
                if two:
                    xT(3)
                if main:
                    rhi(1, 0)
                if two:
                    bandhi(7)
                    yhalf(p2, 0)
                if main:
                    rhi(1, 1)
                    sig_hi(nxt, 2, 1)
                    rhi(1, 2)

            def prepare():
                act.wait_ge(corners, 4)
                act.wait_ge(vt_done, 2)
                for g in range(2):
                    rows = slice(64 * g, 64 * g + 64)
                    for k, (t0, t1) in enumerate(((0, 5), (5, 9))):
                        copy(v2_hi[rows, t0:t1, rows], v2_of(rows, k)).then_inc(v_hi_done, 1)
                    copy(v3_hi[rows, g, :], psR[1][rows, C:2 * C]).then_inc(v_hi_done, 1)

            each_step(act, step, prepare)

            def root(i, k):
                act.wait_ge(bn_dve, k)
                act.activation(mv[:, 8:10], mv[:, 6:8], ACT.Sqrt).then_inc(bn_act, 1)

            root(1, BN1_ROOT)
            act.wait_ge(bn_dve, BN1_END)
            act.wait_ge(borders, 8)
            for i in range(8):
                act.wait_ge(y_loaded[0], 16 * 8)
                act.wait_ge(y_loaded[1], 16 * 8)
                act.activation(y[:, i, :], y[:, i, :], ACT.Relu, bias=shift[:, 0:1], scale=scale[:, 0:1]).then_inc(relu1, 1)
                act.wait_ge(relu1, i + 1)
                copy(h1_hi[:, i // 4, i % 4, 1:SH + 1, 1:SW + 1],
                     y[:, i, :].rearrange("p (r c) -> p r c", c=SW)).then_inc(h1_hi_done, 1)
            act.wait_ge(h1_lo_done, 8)
            for k in range(16):
                act.wait_ge(c2_done, k + 1)
                copy(y[:, k // 2, (k % 2) * HALF:(k % 2 + 1) * HALF], ps[:, k % 8, :]).then_inc(c2_copied, 1)
            root(2, BN2_ROOT)
            act.wait_ge(bn_dve, BN2_END)
            for i in range(8):
                if i == 0:
                    act.wait_ge(c2_copied, 16)
                act.activation(y[:, i, :], y[:, i, :], ACT.Relu, bias=shift[:, 1:2], scale=scale[:, 1:2]).then_inc(relu2, 1)
                act.wait_ge(relu2, i + 1)
                copy(h2_hi[:, i, :], y[:, i, :]).then_inc(h2_hi_done, 1)
            root(3, BN3_ROOT)
            act.wait_ge(bn_dve, BN3_END)
            for u in range(8):
                cb = u % 2
                for k in range(8):
                    h, a, b = k // 4, (k // 2) % 2, k % 2
                    act.wait_ge(f_added, 8 * u + k + 1)
                    if u >= 2 and k % 4 == 0:
                        act.wait_ge(out_stored[u % 2], 16 * (2 * (u // 2 - 1) + 2))
                    act.activation(outs[u % 2][:, 32 * h + a:32 * h + 32:2, b::2],
                                   x1in[:, u % 4, 2 * a + b, h * HALF:(h + 1) * HALF].rearrange("p (r c) -> p r c", c=SW),
                                   ACT.Relu, bias=shift[:, 2 + cb:3 + cb]).then_inc(f_out, 1)

        @block.tensor
        def _(pe):
            def mm3(dst, l_hi, l_lo, r_hi_, r_lo_, first, last, **kw):
                pe.matmul(dst, l_hi, r_hi_, start=first, stop=False, **kw)
                pe.matmul(dst, l_hi, r_lo_, start=False, stop=False, **kw)
                return pe.matmul(dst, l_lo, r_hi_, start=False, stop=last, **kw)

            pe.wait_ge(masked, 7)
            pe.wait_ge(small_loaded, 64)
            pe.transpose(psU[:, 0:KK], w2raw[:, :], ident[0:KK, 0:KK]).then_inc(prep_pe, 1)
            for kb in range(CB):
                pe.transpose(psT[:, kb * MID1:(kb + 1) * MID1], v1raw[:, kb * P:(kb + 1) * P],
                             ident[0:MID1, 0:MID1]).then_inc(prep_pe, 1)
            pe.wait_ge(prep_dve, 1)
            pe.matmul(psXT[0:KK, 0:1], w2T[:, :], b1s[:, :], start=True, stop=True).then_inc(prep_pe, 1)
            for i in range(CB * K):
                kb, v = i // K, i % K
                if v == 0:
                    pe.wait_ge(w1_loaded[kb], 16)
                if i >= 2:
                    pe.wait_ge(wlo_done, i - 1)
                for u in range(K):
                    mm = pe.matmul(psR[i % 2][:, u * KK:(u + 1) * KK], w1raw[:, kb, :, u * K + v], w2T[:, :],
                                   start=True, stop=True)
                mm.then_inc(weff_done, 1)
            pe.wait_ge(wlo_done, CB * K)
            pe.wait_ge(wsum_lo_done, 3 * CB)
            pe.wait_ge(sel_ready, 1)

            def step(n, q):
                s, p1, p2, p3 = (Step(n, q, d) for d in range(4))

                def conv(start, end):
                    for i in range(start, end):
                        g, cb, j = TRIPLES[i]
                        prod, m = GROUPS[g]
                        first, last = (cb, j) == (0, 0), (cb, j) == (CB - 1, TAPS[prod] - 1)
                        if first:
                            if g == 0:
                                pe.wait_ge(sig_lo_done, s.count(6, 3))
                            if g == 3:
                                pe.wait_ge(sig_lo_done, s.count(6, 5))
                            if g in (2, 3, 4):
                                pe.wait_ge(middle_done, s.count(3, g - 2))
                            elif g > 4:
                                pe.wait_ge(outputs_done, s.count(6, g - 5))
                            elif s.live(1):
                                pe.wait_ge(outputs_done, p1.count(6, g + 4))
                        w = weight_of(prod, j)
                        rows = slice(MB * m, MB * m + MS[m])
                        cols = slice(j, j + SW // 2)
                        if prod == ODD:
                            hi, lo = odd_hi[:, s.b, cb, :, cols], odd_lo[:, s.b, cb, :, cols]
                        else:
                            hi, lo = (t[:, cb, :, cols] for t in ((mid_hi, mid_lo) if prod == MIDDLE else (even_hi, even_lo)))
                        mm = mm3(psR[(g + s.b) % 2][0:MS[m], :], w_hi[:, cb, w, rows], w_lo[:, cb, w, rows], hi, lo,
                                 first, last)
                        if last:
                            mm.then_inc(group_done, 1)

                def usum(h):
                    if h == 0:
                        pe.wait_ge(r_lo_done, p1.count(6, 5))
                        if p1.live(2):
                            pe.wait_ge(y1_done, p3.count(2, 0))
                    elif p1.live(1):
                        pe.wait_ge(attn_done, p2.count(2, 0))
                    bank = psU if h == 0 else psT
                    order = [PAD] + [u for u in range(K) if u != PAD]
                    parts = [(u, m) for u in order for m in range(3)
                             if KK * u < MB * m + MS[m] and KK * (u + 1) > MB * m]
                    for i, (u, m) in enumerate(parts):
                        lo, hi = max(HR * h, PAD - u), min(HR * h + HR, SH + PAD - u)
                        at = SELB - (MB * m - KK * u)
                        for j, r in enumerate((r_hi, r_lo)):
                            mm = pe.matmul(bank[0:KK, (lo - HR * h) * SW:(hi - HR * h) * SW], sel[0:MS[m], at:at + KK],
                                           r[0:MS[m], m, (lo + u - PAD) * SW:(hi + u - PAD) * SW],
                                           start=(i == 0 and j == 0), stop=(i == len(parts) - 1 and j == 1),
                                           skip_group_check=True)
                    mm.then_inc(usum_done, 1)

                def logits_T():
                    pe.wait_ge(logits_done, p1.count(2, 1))
                    pe.sem_inc(pe_gate, 1)
                    for t in range(NT):
                        mm = pe.transpose(psT[:, t * KK:(t + 1) * KK], logits[:, t * P:(t + 1) * P], ident[0:KK, 0:KK])
                    mm.then_inc(lt_done, 1)

                def attn_T(h):
                    bank = psT if h == 0 else psU
                    pe.wait_ge(probs_done, p1.count(1, 0))
                    if h == 1 and p3.live():
                        pe.wait_ge(y1_done, p3.count(2, 1))
                    pe.sem_inc(pe_gate, 1)
                    for t in range(4):
                        mm = pe.transpose(bank[0:KK, t * P:(t + 1) * P], probs[:, 4 * h + t, :], ident[:, :])
                    mm.then_inc(at_done, 1)

                def band_T(last):
                    if not last:
                        pe.wait_ge(attn_loaded, p2.dma(NT, NT - 1))
                        if p2.live(1):
                            pe.wait_ge(band_step, p3.count(NT * K, (NT - 1) * K - 1))
                        for t in range(NT - 1):
                            mm = pe.transpose(psB[:, t * JV:(t + 1) * JV], attn_jv[:, t, :], ident[0:JV, 0:JV])
                    else:
                        pe.wait_ge(xT_lo_done, p2.count(4, 2))
                        mm = pe.transpose(psXT[:, 0:JV], attn_jv[:, NT - 1, :], ident[0:JV, 0:JV])
                    mm.then_inc(bt_done, 1)

                def x_T(pair):
                    if pair % 2 == 0:
                        pe.wait_ge(xq_loaded[pair // 2], n * 64 + 32 * ((q - 2) // 2 + 1))
                    if pair == 3:
                        pe.wait_ge(band_step, p2.count(NT * K, NT * K - 1))
                    elif pair:
                        pe.wait_ge(xT_lo_done, p2.count(4, pair - 1))
                    elif p2.live(1):
                        pe.wait_ge(xT_lo_done, p3.count(4, 3))
                    for t in range(2):
                        r = 4 * (2 * pair + t)
                        for kb in range(CB):
                            mm = pe.transpose(psXT[:, t * C + kb * P:t * C + (kb + 1) * P],
                                              xq[:, kb, r:r + 4, p2.b::2], ident[:, :])
                    mm.then_inc(xt_done, 1)

                def unit(i):
                    h, t = UNITS[i]
                    first = t == TILES[h][0]
                    if first:
                        if h == 1:
                            pe.wait_ge(x1_lo_done, p2.count(4, 1))
                            pe.wait_ge(x1_done, p2.count(4, 1))
                        elif p2.live(1):
                            pe.wait_ge(x1_lo_done, p3.count(4, 3))
                            pe.wait_ge(x1_done, p3.count(4, 3))
                    pe.wait_ge(band_lo_done, p2.count(NT, t))
                    pe.wait_ge(xT_lo_done, p2.count(4, t // 2))
                    lo, hi = window(h, t)
                    win = slice(lo - (4 * t - PAD), hi - (4 * t - PAD))
                    for cb in range(CB):
                        cols = slice(cb * P, (cb + 1) * P)
                        mm = mm3(psX[cb][:, (lo - HR * h) * SW:(hi - HR * h) * SW],
                                 xT_hi[:, t % 4, cols], xT_lo[:, t % 4, cols],
                                 band_hi[:, t % 4, win, :], band_lo[:, t % 4, win, :],
                                 first, t == TILES[h][-1], skip_group_check=True)
                    mm.then_inc(unit_done, 1)

                def proj(p, h):
                    pe.wait_ge(x1_lo_done, p.count(4, 2 * h + 1))
                    if h == 1:
                        if Step(n, q, 1).live():
                            pe.wait_ge(logits_done, p1.count(2, 0))
                    elif p1.live():
                        pe.wait_ge(attn_done, p1.count(2, 1))
                    if h == 1 or p.live(1):
                        pe.wait_ge(y1_done, p.count(2, h) - 1)
                    for cb in range(CB):
                        for j, r in enumerate((x1_hi, x1_lo)):
                            mm = pe.matmul(psU, v1pack[:, cb, :], r[:, cb, :],
                                           start=(cb == 0 and j == 0), stop=(cb == CB - 1 and j == 1))
                    mm.then_inc(y_done, 1)

                main, two, one, three = main_live(n), p2.live(), p1.live(), p3.live()
                if two:
                    band_T(False)
                    x_T(0)
                if main:
                    conv(0, 6)
                if one:
                    usum(0)
                if main:
                    conv(6, 10)
                if one:
                    usum(1)
                if two:
                    x_T(1)
                if main:
                    conv(10, 12)
                if three:
                    proj(p3, 1)
                if main:
                    conv(12, 13)
                if one:
                    logits_T()
                if main:
                    conv(13, 21)
                if two:
                    unit(0)
                if main:
                    conv(21, 27)
                if two:
                    unit(1)
                if main:
                    conv(27, 28)
                if two:
                    x_T(2)
                if main:
                    conv(28, 30)
                if one:
                    attn_T(0)
                if main:
                    conv(30, 34)
                if two:
                    unit(2)
                if main:
                    conv(34, 36)
                if one:
                    attn_T(1)
                if main:
                    conv(36, 38)
                if two:
                    unit(3)
                if main:
                    conv(38, 47)
                if two:
                    unit(4)
                if main:
                    conv(47, 51)
                if two:
                    band_T(True)
                if main:
                    conv(51, 59)
                if two:
                    x_T(3)
                if main:
                    conv(59, 60)
                if two:
                    unit(5)
                if main:
                    conv(60, 62)
                if two:
                    proj(p2, 0)
                    unit(6)
                if main:
                    conv(62, 65)
                if two:
                    unit(7)
                if main:
                    conv(65, 66)
                if two:
                    unit(8)
                    unit(9)

            def prepare():
                pe.wait_ge(v_loaded, 16 * 4)
                pe.wait_ge(outputs_done, 6 * STEPS)
                for k in range(2):
                    for t in range(5 - k):
                        mm = pe.transpose(psR[k][:, t * MID1:(t + 1) * MID1], v2raw[:, :, 5 * k + t::9],
                                          ident[0:MID1, 0:MID1])
                    if k == 1:
                        for cb in range(CB):
                            mm = pe.transpose(psR[1][:, C + cb * P:C + (cb + 1) * P], v3raw[:, cb, :, :], ident[:, :])
                    mm.then_inc(vt_done, 1)

            each_step(pe, step, prepare)

            def average(k, col):
                pe.wait_ge(bn_dve, k)
                pe.matmul(ps[:, 7, 0:1], gavg[:, :], mv[:, col:col + 1], start=True, stop=True).then_inc(bn_pe, 1)

            pe.wait_ge(bn_dve, BN1_STAT)
            pe.matmul(ps[:, 7, 0:2], gavg[0:MID1, :], mv[0:MID1, 0:2], start=True, stop=True).then_inc(bn_pe, 1)
            pe.wait_ge(v_lo_done, 6)
            pe.wait_ge(v_hi_done, 6)
            pe.wait_ge(borders, 8)
            for k in range(16):
                sub, h = k // 2, k % 2
                n2, a, b = sub // 4, (sub // 2) % 2, sub % 2
                if k >= 8:
                    pe.wait_ge(c2_copied, k - 7)
                taps = sorted(range(9), key=lambda t: ((a + t // 3 - 1) % 2) * 2 + (b + t % 3 - 1) % 2)
                for i, t in enumerate(taps):
                    ya, xb = a + t // 3 - 1, b + t % 3 - 1
                    if k % 8 == 0:
                        pe.wait_ge(h1_lo_done, 4 * n2 + (ya % 2) * 2 + xb % 2 + 1)
                    r0, c0 = 1 + HR * h + ya // 2, 1 + xb // 2
                    src = slice(r0, r0 + HR), slice(c0, c0 + SW)
                    mm = mm3(ps[:, k % 8, :], v2_hi[:, t, :], v2_lo[:, t, :],
                             h1_hi[:, n2, (ya % 2) * 2 + xb % 2, src[0], src[1]],
                             h1_lo[:, n2, (ya % 2) * 2 + xb % 2, src[0], src[1]], i == 0, i == 8)
                mm.then_inc(c2_done, 1)
            average(BN2_MEAN, 0)
            average(BN2_VAR, 4)

            def last(k, cb, g, sub, h):
                return mm3(ps[:, k % 8, :], v3_hi[:, g, cb * P:(cb + 1) * P], v3_lo[:, g, cb * P:(cb + 1) * P],
                           h2_hi[:, sub, h * HALF:(h + 1) * HALF], h2_lo[:, sub, h * HALF:(h + 1) * HALF], True, True)

            for k in range(64):
                sub, g, h, cb = k // 8, (k // 4) % 2, (k // 2) % 2, k % 2
                if k % 8 == 0:
                    pe.wait_ge(h2_lo_done, sub + 1)
                if k >= 8:
                    pe.wait_ge(c3_stat, k - 7)
                last(k, cb, g, sub, h).then_inc(c3_done, 1)
            for k in range(64):
                u, h, a, b = k // 8, (k // 4) % 2, (k // 2) % 2, k % 2
                n2, g, cb = u // 4, (u // 2) % 2, u % 2
                if k < 8:
                    pe.wait_ge(c3_stat, 57 + k)
                else:
                    pe.wait_ge(f_added, k - 7)
                last(k, cb, g, 4 * n2 + 2 * a + b, h).then_inc(f_done, 1)

        @block.vector
        def _(dve):
            def minus(dst, a, b):
                return dve.tensor_tensor(dst, a, b, ALU.subtract)

            dve.wait_ge(prep_pe, 1)
            dve.tensor_copy(w2T[:, :], psU[:, 0:KK]).then_inc(prep_dve, 1)
            dve.wait_ge(v1_hi_done, 2)
            for kb in range(CB):
                minus(v1pack[:, kb, MID1:P], psT[:, kb * MID1:(kb + 1) * MID1],
                      v1pack[:, kb, 0:MID1].bitcast(F32)).then_inc(v1_lo_done, 1)
            dve.wait_ge(prep_pe, 4)
            dve.wait_ge(small_loaded, 64)
            dve.tensor_tensor(beff[:, :], psXT[0:KK, 0:1], b2s[:, :], ALU.add).then_inc(prep_dve, 1)
            dve.wait_ge(masked, 9)
            dve.wait_ge(consts, 7)

            def differences(s, piece, cb):
                i = 2 * piece + cb
                if i:
                    dve.wait_ge(sig_lo_done, s.count(6, 1 if i == 4 else i - 1))
                elif s.live(1):
                    dve.wait_ge(sig_lo_done, s.ago(1).count(6, 5))
                k = 1 if piece == 0 else 0
                width = SIGW[ODD] if piece == 0 else SIGW[EVEN]
                minus(diff[:, :, 0:width], phase(s, cb, k, width), phase(s, cb, k + 1, width)).then_inc(diff_done, 1)

            dve.wait_ge(x_loaded, 32)
            for piece in (0, 2):
                for cb in range(CB):
                    differences(Step(0, 0), piece, cb)
            for i in range(CB * K):
                cb, v = i // K, i % K
                k = 3 * cb + v // 2
                dve.wait_ge(whi_done, i + 1)
                if v % 2 == 0 and v < K - 1:
                    dve.wait_ge(wcopy_done, k + 1)
                if v % 2 == 1:
                    if k:
                        dve.wait_ge(wsum_hi_done, k)
                        dve.wait_ge(wsum_lo_done, k)
                    dve.tensor_tensor(wsum[:, :], psR[i % 2][:, 0:UK], wtmp[:, :], ALU.add).then_inc(wsum_done, 1)
                w = v // 2 + 4 * (v % 2)
                minus(w_lo[:, cb, w, :], psR[i % 2][:, 0:UK], w_hi[:, cb, w, :].bitcast(F32)).then_inc(wlo_done, 1)
                if v % 2 == 1:
                    dve.wait_ge(wsum_hi_done, k + 1)
                    minus(w_lo[:, cb, 7 + v // 2, :], wsum[:, :], w_hi[:, cb, 7 + v // 2, :].bitcast(F32)
                          ).then_inc(wsum_lo_done, 1)

            def step(n, q):
                s, p1, p2, p3 = (Step(n, q, d) for d in range(4))
                nxt = Step(n, q, -1)

                def x_out(p, h):
                    for cb in range(CB):
                        dve.wait_ge(x1_done, p.count(4, 2 * h + cb))
                        minus(x1_lo[:, cb, :], psX[cb], x1_hi[:, cb, :].bitcast(F32)).then_inc(x1_lo_done, 1)

                def xT(pair):
                    slots = slice(2 * pair % 4, 2 * pair % 4 + 2)
                    dve.wait_ge(xT_hi_done, p2.count(4, pair))
                    wait_slot(dve, p2, 2 * pair + 1)
                    minus(xT_lo[:, slots, :], psXT.rearrange("p (t c) -> p t c", c=C), xT_hi[:, slots, :].bitcast(F32)
                          ).then_inc(xT_lo_done, 1)

                def build_band(t):
                    dve.wait_ge(bt_done, p2.count(2, t // (NT - 1)))
                    if t >= 2:
                        dve.wait_ge(band_lo_done, p2.count(NT, t - 2))
                    elif p2.live(1):
                        dve.wait_ge(band_lo_done, p3.count(NT, t + 6))
                    w = (psB[:, t * JV:(t + 1) * JV] if t < NT - 1 else psXT[:, 0:JV]).rearrange("p (j v) -> p j v", v=K)[:, ::-1, :]
                    for v in range(K):
                        if v or t or p2.live(1):
                            dve.wait_ge(band_step, p2.count(NT * K, t * K + v) - 1)
                        dve.sem_inc(dve_gate, 1)
                        dve.copy_predicated(band[:, t % 2, :, :],
                                            mask[:, v:v + 1, :].bitcast(U32).to_broadcast([P, WIN, SW]),
                                            w[:, :, v:v + 1].to_broadcast([P, WIN, SW])).then_inc(band_step, 1)

                def filter_out(e, m):
                    g = 3 + 3 * e + m
                    dve.wait_ge(group_done, s.count(NG, g))
                    bank = psR[(g + s.b) % 2][0:MS[m], :]
                    if e == 0:
                        dve.wait_ge(middle_done, s.count(3, m))
                        if m:
                            dve.wait_ge(r_lo_done, s.count(6, m - 1))
                        dve.tensor_tensor(evens[0:MS[m], :], bank, middle[0:MS[m], m, :], ALU.add
                                          ).then_inc(outputs_done, 1)
                    else:
                        minus(middle[0:MS[m], m, :], middle[0:MS[m], m, :], bank).then_inc(outputs_done, 1)

                def softmax_top():
                    dve.wait_ge(lt_done, p1.count(1, 0))
                    lt = psT[:, 0:NT * KK].rearrange("p (t k) -> p t k", k=KK)
                    dve.tensor_reduce(smx[:, 0, :], lt, AX_X, ALU.max).then_inc(max_done, 1)
                    dve.wait_ge(max_done, p1.count(1, 0))
                    if p1.live(1):
                        dve.wait_ge(at_done, p2.count(2, 1))
                    minus(probs[:, :, :], lt, smx[:, 0, :].unsqueeze(2).to_broadcast([P, NT, KK])).then_inc(sub_done, 1)

                def softmax_end():
                    dve.wait_ge(exp_done, p1.count(1, 0))
                    dve.tensor_reduce(smx[:, 1, :], probs[:, :, :], AX_X, ALU.add).then_inc(norm_done, 1)
                    dve.wait_ge(norm_done, p1.count(2, 0))
                    dve.reciprocal(smx[:, 2, :], smx[:, 1, :]).then_inc(norm_done, 1)
                    dve.wait_ge(norm_done, p1.count(2, 1))
                    dve.tensor_tensor(probs[:, :, :], probs[:, :, :],
                                      smx[:, 2, :].unsqueeze(2).to_broadcast([P, NT, KK]), ALU.mult
                                      ).then_inc(probs_done, 1)

                def y_out(p, h):
                    dve.wait_ge(yhalf_done, p.count(2, h))
                    dve.tensor_tensor(y1[:, h, :], psU[0:MID1, :], y1[:, h, :], ALU.add).then_inc(y1_done, 1)
                    dve.wait_ge(y1_done, p.count(2, h))
                    dve.bn_stats(stats1[:, p.n * 8 + (2 * p.k + h), :], y1[:, h, :]).then_inc(y1_stat, 1)

                main, two, one, three = main_live(n), p2.live(), p1.live(), p3.live()
                if two:
                    build_band(0)
                    xT(0)
                if three:
                    x_out(p3, 1)
                if two:
                    build_band(1)
                    build_band(2)
                if main:
                    if q % 2 == 1:
                        dve.wait_ge(x_loaded, n * 64 + 32 * ((q + 1) // 2 + 1))
                    differences(nxt, 0, 0)
                if one:
                    softmax_top()
                if main:
                    differences(nxt, 0, 1)
                if two:
                    xT(1)
                    build_band(3)
                if one:
                    softmax_end()
                if two:
                    build_band(4)
                if three:
                    y_out(p3, 1)
                if two:
                    build_band(5)
                    xT(2)
                if main:
                    filter_out(0, 0)
                if two:
                    build_band(6)
                if main:
                    filter_out(0, 1)
                    differences(nxt, 2, 0)
                    filter_out(0, 2)
                if two:
                    build_band(7)
                    x_out(p2, 0)
                if main:
                    filter_out(1, 0)
                if two:
                    xT(3)
                if main:
                    differences(nxt, 2, 1)
                    filter_out(1, 1)
                if two:
                    y_out(p2, 0)
                if main:
                    filter_out(1, 2)

            def prepare():
                for g in range(2):
                    rows = slice(64 * g, 64 * g + 64)
                    for k, (t0, t1) in enumerate(((0, 5), (5, 9))):
                        dve.wait_ge(v_hi_done, 6)
                        minus(v2_lo[rows, t0:t1, rows], v2_of(rows, k), v2_hi[rows, t0:t1, rows].bitcast(F32)
                              ).then_inc(v_lo_done, 1)
                    minus(v3_lo[rows, g, :], psR[1][rows, C:2 * C], v3_hi[rows, g, :].bitcast(F32)).then_inc(v_lo_done, 1)

            each_step(dve, step, prepare)

            done = [0]

            def link(op):
                done[0] += 1
                op.then_inc(bn_dve, 1)
                dve.wait_ge(bn_dve, done[0])

            def affine(i, width, var, mean, gamma, beta, roots):
                link(dve.tensor_scalar(mv[:, 6:8], var, EPS, None, ALU.add))
                dve.wait_ge(bn_act, roots)
                sc, sh = scale[:, i:i + width], shift[:, i:i + width]
                link(dve.reciprocal(mv[:, 10:12], mv[:, 8:10]))
                link(dve.tensor_tensor(sc, mv[:, 10:10 + width], gamma, ALU.mult))
                link(dve.tensor_tensor(mv[:, 12:12 + width], mean, sc, ALU.mult))
                link(dve.tensor_tensor(sh, beta, mv[:, 12:12 + width], ALU.subtract))

            def norm(i, pes):
                link(dve.bn_aggr(mv[:, 0:2], stats[:, :, :].rearrange("p k e -> p (k e)")))
                dve.wait_ge(bn_pe, pes)
                link(dve.tensor_copy(mv[:, 2:3], ps[:, 7, 0:1]))
                link(dve.tensor_tensor(mv[:, 3:4], mv[:, 0:1], mv[:, 2:3], ALU.subtract))
                link(dve.scalar_tensor_tensor(out=mv[:, 4:5], in0=mv[:, 3:4], scalar=mv[:, 3:4], in1=mv[:, 1:2],
                                              op0=ALU.mult, op1=ALU.add))
                dve.wait_ge(bn_pe, pes + 1)
                link(dve.tensor_copy(mv[:, 5:6], ps[:, 7, 0:1]))
                affine(i, 1, mv[:, 5:6].to_broadcast([P, 2]), mv[:, 2:3], bn[:, 2 * i:2 * i + 1],
                       bn[:, 2 * i + 1:2 * i + 2], i + 1)

            dve.wait_ge(bn_loaded, 16 * 12)
            dve.wait_ge(y1_stat, 2 * STEPS)
            dve.wait_ge(x1_stored[0], 16 * STEPS)
            dve.wait_ge(x1_stored[1], 16 * STEPS)
            link(dve.bn_aggr(mv[0:MID1, 0:2], stats1[:, :, :].rearrange("p k e -> p (k e)")))
            dve.wait_ge(bn_pe, 1)
            link(dve.tensor_scalar(mv[:, 2:4], ps[:, 7, 0:2], 2.0, None, ALU.mult))
            affine(0, 1, mv[:, 3:4].to_broadcast([P, 2]), mv[:, 2:3], bn[:, 0:1], bn[:, 1:2], 1)
            for i in range(8):
                dve.wait_ge(h1_hi_done, i + 1)
                minus(h1_lo[:, i // 4, i % 4, 1:SH + 1, 1:SW + 1], y[:, i, :].rearrange("p (r c) -> p r c", c=SW),
                      h1_hi[:, i // 4, i % 4, 1:SH + 1, 1:SW + 1].bitcast(F32)).then_inc(h1_lo_done, 1)
            for k in range(16):
                dve.wait_ge(c2_copied, k + 1)
                dve.bn_stats(stats[:, k, :], y[:, k // 2, (k % 2) * HALF:(k % 2 + 1) * HALF]).then_inc(c2_stat, 1)
            dve.wait_ge(c2_stat, 16)
            norm(1, 2)
            for i in range(8 + 1):
                if i < 8:
                    dve.wait_ge(h2_hi_done, i + 1)
                    minus(h2_lo[:, i, :], y[:, i, :], h2_hi[:, i, :].bitcast(F32)).then_inc(h2_lo_done, 1)
                for k in range(8 * i - 8, 8 * i):
                    if k >= 0:
                        dve.wait_ge(c3_done, k + 1)
                        dve.bn_stats(stats3[:, k % 2, k // 2, :], ps[:, k % 8, :]).then_inc(c3_stat, 1)
            dve.wait_ge(c3_stat, 64)
            for cb in range(CB):
                link(dve.bn_aggr(mv[:, 2 * cb:2 * cb + 2], stats3[:, cb, :, :].rearrange("p k e -> p (k e)")))
            affine(2, 2, mv[:, 1:4:2], mv[:, 0:4:2], bn[:, 4:6], bn[:, 6:8], 3)
            for k in range(64):
                u, h, sub = k // 8, (k // 4) % 2, k % 4
                cb = u % 2
                if k % 8 == 0:
                    dve.wait_ge(x1_back[u % 4], 16 * (u // 4 + 1))
                dve.wait_ge(f_done, k + 1)
                part = x1in[:, u % 4, sub, h * HALF:(h + 1) * HALF]
                dve.scalar_tensor_tensor(out=part, in0=ps[:, k % 8, :], scalar=scale[:, 2 + cb:3 + cb], in1=part,
                                         op0=ALU.mult, op1=ALU.add).then_inc(f_added, 1)


BN1_STAT, BN1_ROOT, BN1_END = 1, 3, 7
BN2_MEAN, BN2_VAR, BN2_ROOT, BN2_END = 8, 11, 13, 17
BN3_ROOT, BN3_END = 20, 24

_INS = ["x", "L0_conv_w1", "L0_conv_b1", "L0_conv_w2", "L0_conv_b2", "L1_conv_w1", "L1_conv_g1", "L1_conv_b1",
        "L1_conv_w2", "L1_conv_g2", "L1_conv_b2", "L1_conv_w3", "L1_conv_g3", "L1_conv_b3"]


def kernel(**inputs):
    import concourse.bacc as bacc
    from concourse.bass_utils import run_bass_kernel_spmd

    nc = bacc.Bacc("TRN2", target_bir_lowering=False, num_devices=1, dynamic_dma_scratch_size=1024)
    arrays, args = {}, []
    for name in _INS:
        a = np.ascontiguousarray(inputs[name])
        arrays[f"in_{name}"] = a
        args.append(nc.dram_tensor(f"in_{name}", a.shape, mybir.dt.from_np(a.dtype), kind="ExternalInput").ap())
    args.append(nc.dram_tensor("out_0", (B, C, H, W), F32, kind="ExternalOutput").ap())
    build(nc, *args)
    r = run_bass_kernel_spmd(nc, [arrays], core_ids=[0])
    return r.results[0]["out_0"]
```

```python
from contextlib import ExitStack

import numpy as np

import concourse.bass as bass
from concourse import mybir

F32 = mybir.dt.float32
F32R = mybir.dt.float32r
U32 = mybir.dt.uint32
ALU = mybir.AluOpType
ACT = mybir.ActivationFunctionType
AX_X = mybir.AxisListType.X

P = 128
B, C, H, W = 4, 256, 64, 64
CB = C // P
K = 7
KK = K * K
MID0 = 128
SH, SW = H // 2, W // 2
SPX = SH * SW
HALF = SPX // 2
HR = SH // 2
PAD = K // 2
PW = SW + 2 * PAD
PH = SH + 2 * PAD
PLANE = PH * PW
UPLANES = K * (PLANE - 1) + PW
PLANES = (2 * K - 1) * UPLANES
UK = K * KK
MB = 115
MS = [MB, MB, UK - 2 * MB]
NT = SH // 4
WIN = 4 + 2 * PAD
JV = WIN * K
MID1 = 64
STEPS = 4 * B
EPS = 1e-5
SELW = 2 * KK
PARITY = HALF
SIG0 = 5
H2_DVE = 2
X1_SLOTS = 6
LAG = 3


def window(h, t):
    return max(4 * t - PAD, HR * h), min(4 * t + 4 + PAD, HR * h + HR)


MIDDLE, EVEN, ODD = 0, 1, 2
TAPS = {MIDDLE: (K + 1) // 2, EVEN: (K + 1) // 2, ODD: K // 2}
SIGW = {MIDDLE: SW // 2 + 3, EVEN: SW // 2 + 3, ODD: SW // 2 + 2}
GROUPS = [(prod, m) for prod in (MIDDLE, EVEN, ODD) for m in range(3)]
TRIPLES = [(g, cb, j) for g, (prod, m) in enumerate(GROUPS) for cb in range(CB) for j in range(TAPS[prod])]
NG = len(GROUPS)
NW = 10


def weight_of(prod, j):
    if prod == MIDDLE and j < K // 2:
        return 7 + j
    return 4 + j if prod == ODD else j


TILES = [[t for t in range(NT) if window(h, t)[0] < window(h, t)[1]] for h in range(2)]
UNITS = [(h, t) for h in range(2) for t in TILES[h]]


def build(nc, x, w1, b1, w2, b2, v1, g1, c1, v2, g2, c2, v3, g3, c3, out):
    attn_planes = nc.dram_tensor("attn_planes", (2, PLANES), F32, kind="Internal").ap()
    x1_dram = nc.dram_tensor("x1_dram", (STEPS, CB, P, SPX), F32, kind="Internal").ap()
    y1_dram = nc.dram_tensor("y1_dram", (STEPS, MID1, SPX), F32, kind="Internal").ap()

    top = ExitStack()
    with top:
        def sem(name):
            return top.enter_context(nc.semaphore(name))

        def sb(stack, name, shape, dt=F32):
            return stack.enter_context(nc.sbuf_tensor(name, shape, dt))

        ps = top.enter_context(nc.psum_tensor("ps", [P, 8, 512], F32))
        psR = [ps[:, 0, :], ps[:, 1, :]]
        psX = [ps[:, 2, :], ps[:, 3, :]]
        psU, psT, psXT, psB = ps[:, 4, :], ps[:, 5, :], ps[:, 6, :], ps[:, 7, :]

        ident = sb(top, "ident", [P, P])
        gavg = sb(top, "gavg", [P, P])
        stats1 = sb(top, "stats1", [MID1, 2 * STEPS, 6])
        bn = sb(top, "bn", [P, 8])

        l0 = ExitStack()
        w_hi = sb(l0, "w_hi", [P, CB, NW, UK], F32R)
        w_lo = sb(l0, "w_lo", [P, CB, NW, UK], F32R)
        xraw = sb(l0, "xraw", [P, CB, SH, W + 4 * PAD])
        mid_hi = sb(l0, "mid_hi", [P, CB, SH, SIGW[MIDDLE]], F32R)
        mid_lo = sb(l0, "mid_lo", [P, CB, SH, SIGW[MIDDLE]], F32R)
        even_hi = sb(l0, "even_hi", [P, CB, SH, SIGW[EVEN]], F32R)
        even_lo = sb(l0, "even_lo", [P, CB, SH, SIGW[EVEN]], F32R)
        odd_hi = sb(l0, "odd_hi", [P, 2, CB, SH, SIGW[ODD]], F32R)
        odd_lo = sb(l0, "odd_lo", [P, 2, CB, SH, SIGW[ODD]], F32R)
        diff = sb(l0, "diff", [P, SH, SIGW[EVEN]])
        middle = sb(l0, "middle", [P, 3, HALF])
        evens = sb(l0, "evens", [P, HALF])
        r_split = sb(l0, "r_split", [P, 2, PARITY], F32R)
        r_moved = sb(l0, "r_moved", [P, 3, 2, 2, PARITY], F32R)
        l0r = ExitStack()
        sel = sb(l0r, "sel", [P, SELW], F32R)
        mask = sb(l0r, "mask", [P, K, SW])
        v1pack = sb(l0r, "v1pack", [P, CB, P], F32R)
        band = sb(l0r, "band", [P, 4, WIN, SW])
        beff = sb(l0r, "beff", [KK, 1])
        w2T = sb(l0r, "w2T", [P, KK])
        b1s = sb(l0r, "b1s", [P, 1])
        b2s = sb(l0r, "b2s", [KK, 1])
        l0a = ExitStack()
        w1raw = sb(l0a, "w1raw", [P, CB, P, KK])
        w2raw = sb(l0a, "w2raw", [KK, P])
        v1raw = sb(l0a, "v1raw", [MID1, C])
        zeros = sb(l0a, "zeros", [P, 1024])
        self32 = sb(l0a, "self32", [P, SELW])
        wtmp = sb(l0a, "wtmp", [P, UK])
        wsum = sb(l0a, "wsum", [P, UK])
        l0a.close()
        l0b = ExitStack()
        attn = sb(l0b, "attn", [KK, SPX])
        probs = sb(l0b, "probs", [P, NT, KK])
        smx = sb(l0b, "smx", [P, 3, NT])
        attn_jv = sb(l0b, "attn_jv", [JV, NT, P])
        xq = sb(l0b, "xq", [P, CB, SH, W])
        xT_hi = sb(l0b, "xT_hi", [P, 4, C], F32R)
        xT_lo = sb(l0b, "xT_lo", [P, 4, C], F32R)
        band_hi = sb(l0b, "band_hi", [P, 4, WIN, SW], F32R)
        band_lo = sb(l0b, "band_lo", [P, 4, WIN, SW], F32R)
        x1 = sb(l0b, "x1", [P, CB, HALF])
        x1_hi = sb(l0b, "x1_hi", [P, CB, HALF], F32R)
        x1_lo = sb(l0b, "x1_lo", [P, CB, HALF], F32R)
        y1 = sb(l0b, "y1", [MID1, 2, HALF])
        l0b.close()
        l0r.close()
        l0.close()

        l1 = ExitStack()
        y = sb(l1, "y", [P, 8, SPX])
        v2_hi = sb(l1, "v2_hi", [P, 6, P], F32R)
        v2_lo = sb(l1, "v2_lo", [P, 6, P], F32R)
        v3_hi = sb(l1, "v3_hi", [P, 2, C], F32R)
        v3_lo = sb(l1, "v3_lo", [P, 2, C], F32R)
        v3raw = sb(l1, "v3raw", [P, CB, 2, MID1])
        v2raw = sb(l1, "v2raw", [MID1, 2, MID1 * 9])
        stats = sb(l1, "stats", [P, 16, 6])
        mv = sb(l1, "mv", [P, 16])
        scale = sb(l1, "scale", [P, 4])
        shift = sb(l1, "shift", [P, 4])
        h2s = ExitStack()
        h2_hi = sb(h2s, "h2_hi", [P, 8, SPX], F32R)
        h2_lo = sb(h2s, "h2_lo", [P, 8, SPX], F32R)
        stats3 = sb(h2s, "stats3", [P, CB, 32, 6])
        h2s.close()
        h1_hi = sb(l1, "h1_hi", [P, B, 2, SH + 1, SW + 2], F32R)
        h1_lo = sb(l1, "h1_lo", [P, B, 2, SH + 1, SW + 2], F32R)
        x1in = sb(l1, "x1in", [P, X1_SLOTS, 4, SPX])
        l1.close()
        outs = [y[:, 4 * k:4 * k + 4, :].rearrange("p i e -> p (i e)").rearrange("p (r c) -> p r c", c=W) for k in range(2)]

        zeroed, consts, masked, sel_ready = sem("zeroed"), sem("consts"), sem("masked"), sem("sel_ready")
        small_loaded, bn_loaded, w1_loaded = sem("small_loaded"), sem("bn_loaded"), [sem("w1_loaded0"), sem("w1_loaded1")]
        planes_zero = sem("planes_zero")
        prep_pe, prep_dve = sem("prep_pe"), sem("prep_dve")
        weff_done, whi_done, wlo_done = sem("weff_done"), sem("whi_done"), sem("wlo_done")
        v1_hi_done, v1_lo_done = sem("v1_hi_done"), sem("v1_lo_done")
        wcopy_done, wsum_done, wsum_hi_done, wsum_lo_done = sem("wcopy_done"), sem("wsum_done"), sem("wsum_hi_done"), sem("wsum_lo_done")
        x_loaded, diff_done, sig_hi_done, sig_lo_done = sem("x_loaded"), sem("diff_done"), sem("sig_hi_done"), sem("sig_lo_done")
        group_done, middle_done, outputs_done = sem("group_done"), sem("middle_done"), sem("outputs_done")
        r_hi_done, r_lo_done = sem("r_hi_done"), sem("r_lo_done")
        moved_zero, r_in = sem("moved_zero"), [sem("r_in0"), sem("r_in1")]
        usum_done, logits_done, lt_done = sem("usum_done"), sem("logits_done"), sem("lt_done")
        max_done, sub_done, exp_done = sem("max_done"), sem("sub_done"), sem("exp_done")
        norm_done, probs_done = sem("norm_done"), sem("probs_done")
        at_done, attn_done, attn_stored, attn_loaded = sem("at_done"), sem("attn_done"), sem("attn_stored"), sem("attn_loaded")
        bt_done, band_step, band_hi_done, band_lo_done = sem("bt_done"), sem("band_step"), sem("band_hi_done"), sem("band_lo_done")
        xq_loaded = [sem("xq_loaded0"), sem("xq_loaded1")]
        xt_done, xT_hi_done, xT_lo_done = sem("xt_done"), sem("xT_hi_done"), sem("xT_lo_done")
        unit_done, x1_hi_done, x1_done, x1_lo_done = sem("unit_done"), sem("x1_hi_done"), sem("x1_done"), sem("x1_lo_done")
        y_done, yhalf_done, y1_done = sem("y_done"), sem("yhalf_done"), sem("y1_done")
        y1_stat = sem("y1_stat")
        x1_stored, y1_stored = [sem("x1_stored0"), sem("x1_stored1")], sem("y1_stored")
        v_loaded = sem("v_loaded")
        y_loaded = [sem("y_loaded0"), sem("y_loaded1")]
        borders, corners = sem("borders"), sem("corners")
        vt_done, v_hi_done, v_lo_done = sem("vt_done"), sem("v_hi_done"), sem("v_lo_done")
        dve_gate, pe_gate, sp_gate = sem("dve_gate"), sem("pe_gate"), sem("sp_gate")
        bn_dve, bn_pe, bn_act = sem("bn_dve"), sem("bn_pe"), sem("bn_act")
        relu1, h1_hi_done, h1_lo_done = sem("relu1"), sem("h1_hi_done"), sem("h1_lo_done")
        relu2, h2_hi_done, h2_lo_done, h2_lo_pool = sem("relu2"), sem("h2_hi_done"), sem("h2_lo_done"), sem("h2_lo_pool")
        c2_done, c2_copied, c2_stat = sem("c2_done"), sem("c2_copied"), sem("c2_stat")
        c3_done, c3_stat = sem("c3_done"), sem("c3_stat")
        f_done, f_added, f_out = sem("f_done"), sem("f_added"), sem("f_out")
        x1_back = [sem(f"x1_back{k}") for k in range(X1_SLOTS)]
        out_stored = [sem("out_stored0"), sem("out_stored1")]

        class Step:

            def __init__(self, n, q, back=0):
                self.n, self.q, self.back = n, q, back
                self.k = q - back
                self.b = self.k % 2
                self.a = (self.k // 2) % 2

            def live(self, ago=0):
                return not isinstance(self.n, int) or 0 <= 4 * self.n + self.k - ago < STEPS

            def count(self, per_step, i):
                return self.n * (4 * per_step) + (self.k * per_step + i + 1)

            def dma(self, per_step, i):
                return self.n * (64 * per_step) + 16 * (self.k * per_step + i + 1)

            def index(self):
                return self.n * 4 + self.k

            def image(self):
                return self.n + self.k // 4

            def ago(self, m):
                return Step(self.n, self.q, self.back + m)

        def each_step(eng, step, prepare=None):
            for q in range(4):
                step(0, q)
            with eng.Fori(1, B) as n:
                for q in range(4):
                    step(n, q)
            for q in range(LAG):
                step(B, q)
                if q == 0 and prepare:
                    prepare()

        def main_live(n):
            return not isinstance(n, int) or n < B

        def band_event(t, v):
            return 2 * K * (t // 2) + 2 * v + t % 2

        block = top.enter_context(nc.Block())

        def h1_part(h1, i, a):
            return h1[64 * a:64 * a + 64, i // 2, i % 2, a:a + SH, 1:SW + 1]

        def y_part(i, a):
            return y[64 * a:64 * a + 64, i, :].rearrange("p (r c) -> p r c", c=SW)

        def store_out(sp, u):
            n, cb = u // 2, u % 2
            for h in range(2):
                sp.wait_ge(f_out, 8 * u + 4 * h + 4)
                sp.dma_start(out[n, cb * P:(cb + 1) * P, 32 * h:32 * h + 32, :],
                             outs[u % 2][:, 32 * h:32 * h + 32, :]).then_inc(out_stored[u % 2], 16)

        def load_rows(sp, dst, n, a, done, r0=0, r1=SH):
            for cb in range(CB):
                src = x[n, cb * P:(cb + 1) * P].rearrange("p (r a) w -> p r a w", a=2)[:, r0:r1, a, :]
                sp.dma_start(dst[:, cb, r0:r1, :], src).then_inc(done, 16)

        def signal(s, piece, cb):
            if piece == 1:
                return mid_hi[:, cb, :, :], mid_lo[:, cb, :, :], phase(s, cb, 1, SIGW[MIDDLE])
            if piece == 0:
                return odd_hi[:, s.b, cb, :, :], odd_lo[:, s.b, cb, :, :], diff[:, :, 0:SIGW[ODD]]
            return even_hi[:, cb, :, :], even_lo[:, cb, :, :], diff[:, :, 0:SIGW[EVEN]]

        def phase(s, cb, k, width):
            first = 2 * k + s.b
            return xraw[:, cb, :, first:first + 4 * width - 3:4]

        def pieces(m):
            return [(u, max(KK * u - MB * m, 0), min(KK * (u + 1) - MB * m, MS[m])) for u in range(K)
                    if KK * u < MB * m + MS[m] and KK * (u + 1) > MB * m]

        def r_events(s, i):
            return s.dma(9, 3 * (i % 3) + 2)

        def filtered(m, e):
            return evens[0:MS[m], :] if e == 0 else middle[0:MS[m], m, :]

        def v2_of(rows, ty):
            at = (ty % 2) * 3 * MID1
            return psR[ty // 2][rows, at:at + 3 * MID1].rearrange("p (t m) -> p t m", m=MID1)

        def v2_blocks(v):
            even, odd = slice(0, MID1), slice(MID1, P)
            return [(v[even, 0:3, even], 1), (v[even, 0:3, odd], 0), (v[even, 3:6, odd], 2),
                    (v[odd, 0:3, even], 0), (v[odd, 3:6, even], 2), (v[odd, 3:6, odd], 1)]

        def last_unit(t):
            return max(i for i, (h, tt) in enumerate(UNITS) if tt == t)

        def wait_slot(eng, p, t):
            if t >= 4:
                eng.wait_ge(unit_done, p.count(len(UNITS), last_unit(t - 4)))
            elif p.live(1):
                eng.wait_ge(unit_done, p.ago(1).count(len(UNITS), last_unit(t + 4)))

        @block.sync
        def _(sp):
            sp.dma_start(w2raw[:, :], w2.rearrange("k o a b -> k (o a b)")).then_inc(small_loaded, 16)
            sp.dma_start(v1raw[:, :], v1.rearrange("m c a b -> m (c a b)")).then_inc(small_loaded, 16)
            sp.dma_start(b1s[:, :], b1.rearrange("(p a) -> p a", a=1)).then_inc(small_loaded, 16)
            sp.dma_start(b2s[:, :], b2.rearrange("(p a) -> p a", a=1)).then_inc(small_loaded, 16)
            for kb in range(CB):
                sp.dma_start(w1raw[:, kb, :, :].rearrange("p c t -> p (c t)"),
                             w1[:, kb * P:(kb + 1) * P, :, :].rearrange("o c u v -> o (c u v)")
                             ).then_inc(w1_loaded[kb], 16)
                if kb == 0:
                    load_rows(sp, xraw[:, :, :, 2 * PAD:2 * PAD + W], 0, 0, x_loaded)
            sp.wait_ge(zeroed, 1)
            total = 2 * PLANES
            flat = attn_planes.rearrange("s e -> (s e)")
            whole = total // (P * 1024)
            for i in range(whole):
                sp.dma_start(flat[i * P * 1024:(i + 1) * P * 1024].rearrange("(p e) -> p e", p=P),
                             zeros[:, :]).then_inc(planes_zero, 16)
            rest = total - whole * P * 1024
            rows = rest // 1024
            sp.dma_start(flat[whole * P * 1024:(whole * P + rows) * 1024].rearrange("(p e) -> p e", p=rows),
                         zeros[0:rows, :]).then_inc(planes_zero, 16)
            tail = rest - rows * 1024
            if tail:
                sp.dma_start(flat[total - tail:total].rearrange("(p e) -> p e", p=1),
                             zeros[0:1, 0:tail]).then_inc(planes_zero, 16)
            for g in range(2):
                for i, t in enumerate((g1, c1, g2, c2)):
                    sp.dma_start(bn[64 * g:64 * g + 64, i:i + 1], t.rearrange("(p a) -> p a", a=1)).then_inc(bn_loaded, 16)
            for i, t in enumerate((g3, c3)):
                for cb in range(CB):
                    sp.dma_start(bn[:, 4 + 2 * i + cb:5 + 2 * i + cb],
                                 t[cb * P:(cb + 1) * P].rearrange("(p a) -> p a", a=1)).then_inc(bn_loaded, 16)
            sp.wait_ge(planes_zero, 16 * (whole + 1 + bool(tail)))
            sp.wait_ge(moved_zero, 1)

            def step(n, q):
                s, p1, p2, p3 = (Step(n, q, d) for d in range(4))
                at3, at2, following = p3.index(), p2.index(), (n + 1) % B
                if not isinstance(n, int):
                    at3, at2 = sp.snap(at3), sp.snap(at2)
                    following = sp.snap(following) if q == 2 else None

                def move(e, m):
                    sp.wait_ge(r_lo_done, s.count(6, 3 * e + m))
                    if m == 0 and p1.live():
                        sp.sem_inc(sp_gate, 1)
                        sp.wait_ge(usum_done, p1.count(2, e))
                    for u, first, end in pieces(m):
                        r0, r1 = max(0, u - PAD), min(SH, SH + u - PAD)
                        c = SW // 2
                        sp.dma_start(r_moved[first:end, m, :, e, (r0 - u + PAD) * c:(r1 - u + PAD) * c].bitcast(F32),
                                     r_split[first:end, :, r0 * c:r1 * c].bitcast(F32)).then_inc(r_in[e], 16)

                def store_y():
                    sp.wait_ge(y1_done, p3.count(2, 1))
                    sp.dma_start(y1_dram[at3], y1[:, :, :].rearrange("m h e -> m (h e)")).then_inc(y1_stored, 16)

                def store_attn():
                    sp.wait_ge(attn_done, p1.count(2, 1))
                    sp.sem_inc(sp_gate, 1)
                    if p1.live(2):
                        sp.wait_ge(attn_loaded, p1.ago(2).dma(NT, NT - 1))
                    for u in range(K):
                        sp.dma_start(bass.AP(tensor=attn_planes.tensor,
                                             offset=p1.b * PLANES + (PAD + u) * UPLANES + PAD * PW + PAD,
                                             ap=[[PLANE, K], [PW, SH], [1, SW]]),
                                     attn[u * K:(u + 1) * K, :].rearrange("k (r c) -> k r c", c=SW)).then_inc(attn_stored, 16)

                def load_attn():
                    sp.wait_ge(attn_stored, p1.dma(K, K - 1))
                    sp.sem_inc(sp_gate, 1)
                    if p1.live(1):
                        sp.wait_ge(bt_done, p2.count(2, 1))
                    for t in range(NT):
                        src = bass.AP(tensor=attn_planes.tensor,
                                      offset=p1.b * PLANES + (4 * t + WIN - 1) * PW + 2 * PAD,
                                      ap=[[PLANE - 1, JV], [UPLANES, 4], [1, SW]])
                        sp.dma_start(attn_jv[:, t, :], src).then_inc(attn_loaded, 16)

                def load_next():
                    sp.wait_ge(sig_lo_done, s.ago(-1).count(6, 5))
                    sp.sem_inc(sp_gate, 1)
                    load_rows(sp, xraw[:, :, :, 2 * PAD:2 * PAD + W], n if q == 0 else following, 1 if q == 0 else 0,
                              x_loaded)

                main, two, one, three = main_live(n), p2.live(), p1.live(), p3.live()
                even, odd = main and q % 2 == 0, main and q % 2 == 1
                if main:
                    move(0, 0)
                    move(0, 1)
                if odd:
                    load_xq(n, s, p2, 0)
                if three:
                    store_x1(at3, p3, 1)
                if one:
                    store_attn()
                if main:
                    move(0, 2)
                if three:
                    store_y()
                if one:
                    load_attn()
                if two:
                    store_x1(at2, p2, 0)
                if main:
                    move(1, 0)
                if odd:
                    load_xq(n, s, p2, 1)
                if even:
                    load_next()
                if main:
                    move(1, 1)
                    move(1, 2)

            def store_x1(at, p, h):
                sp.wait_ge(x1_done, p.count(4, 2 * h + 1))
                sp.dma_start(x1_dram[at][:, :, h * HALF:(h + 1) * HALF].rearrange("b p e -> p b e"),
                             x1[:, :, :]).then_inc(x1_stored[h], 16)

            def load_xq(n, s, p2, half):
                if p2.live():
                    sp.wait_ge(xt_done, p2.count(4, 1 if half == 0 else 3))
                    sp.sem_inc(sp_gate, 1)
                else:
                    sp.wait_ge(group_done, 1)
                load_rows(sp, xq, n, s.a, xq_loaded[half], half * HR, half * HR + HR)

            def prepare():
                sp.wait_ge(group_done, NG * STEPS)
                sp.wait_ge(usum_done, 2 * STEPS)
                sp.wait_ge(r_lo_done, 6 * STEPS)
                sp.wait_ge(sig_lo_done, 6 * (STEPS + 1))
                for g in range(2):
                    sp.dma_start(v3raw[:, :, g, :], v3.rearrange("(b p) m x y -> p b (m x y)", p=P)).then_inc(v_loaded, 16)
                    sp.dma_start(v2raw[:, g, :], v2.rearrange("o i y x -> o (i y x)")).then_inc(v_loaded, 16)
                for i in range(STEPS - LAG + 1):
                    load_y(i, 0)

            def load_y(i, last):
                n, a, b = i // 4, (i // 2) % 2, i % 2
                sp.wait_ge(y1_stored, 16 * (i + 1))
                sp.dma_start(y[64 * a:64 * a + 64, 2 * n + b, :], y1_dram[i]).then_inc(y_loaded[last], 16)

            each_step(sp, step, prepare)

            for i in range(STEPS - LAG + 1, STEPS):
                load_y(i, 1)
            for h in range(2):
                sp.wait_ge(x1_stored[h], 16 * STEPS)

            def load_x1(u):
                n, cb = u // 2, u % 2
                sp.dma_start(x1in[:, u % X1_SLOTS, :, :], x1_dram[4 * n:4 * n + 4, cb].rearrange("s p e -> p s e")
                             ).then_inc(x1_back[u % X1_SLOTS], 16)

            sp.wait_ge(y1_stat, 2 * STEPS)
            for u in range(X1_SLOTS):
                load_x1(u)
            for u in range(8):
                store_out(sp, u)
                if u + X1_SLOTS < 8:
                    load_x1(u + X1_SLOTS)
            for k in range(2):
                sp.wait_ge(out_stored[k], 16 * 8)

        @block.gpsimd
        def _(pool):
            pool.memset(zeros[:, :], 0.0).then_inc(zeroed, 1)
            for t in (ident[:, :], gavg[:, :], self32[:, :], mask[:, :, :]):
                pool.memset(t, 0.0).then_inc(consts, 1)
            for c0 in (0, 2 * PAD + W):
                pool.memset(xraw[:, :, :, c0:c0 + 2 * PAD], 0.0).then_inc(consts, 1)
            pool.memset(band[:, :, :, :], 0.0).then_inc(consts, 1)
            pool.wait_ge(consts, 7)

            puts = [(ident[:, :], 1.0, 0, [[-1, P]], 1), (gavg[:, :], 0.5, 0, [[-1, P]], 1),
                    *((self32[:, :], 1.0, KK * d, [[1, SELW]], -1) for d in range(-1, 3))]
            puts += [(mask[32 * g:32 * g + 32, :, :], 1.0, -PAD, [[1, K], [1, SW]], -1) for g in range(4)]
            puts += [(gavg[:, :], 0.5, d, [[-1, P]], 1) for d in (64, -64)]
            for i, (t, value, base, pattern, per_partition) in enumerate(puts):
                if i:
                    pool.wait_ge(masked, i)
                pool.affine_select(out=t, in_=t, compare_op=ALU.not_equal, fill=value, base=base, pattern=pattern,
                                   channel_multiplier=per_partition).then_inc(masked, 1)
            pool.wait_ge(masked, len(puts))
            pool.memset(r_moved[:, :, :, :, :].bitcast(F32), 0.0).then_inc(moved_zero, 1)

            def sig_lo(s, piece, cb):
                pool.wait_ge(sig_hi_done, s.count(6, 2 * piece + cb))
                hi, lo, src = signal(s, piece, cb)
                pool.tensor_tensor(lo, src, hi.bitcast(F32), ALU.subtract).then_inc(sig_lo_done, 1)

            for i in range(6):
                sig_lo(Step(0, 0), i // 2, i % 2)

            def step(n, q):
                s, p1, p2, p3 = (Step(n, q, d) for d in range(4))
                nxt = Step(n, q, -1)

                def band_tile(t):
                    pool.wait_ge(band_hi_done, p2.count(NT, t))
                    wait_slot(pool, p2, t)
                    pool.tensor_tensor(band_lo[:, t % 4, :, :], band[:, t % 4, :, :],
                                       band_hi[:, t % 4, :, :].bitcast(F32), ALU.subtract
                                       ).then_inc(band_lo_done, 1)

                def rlo(e, m):
                    i = 3 * e + m
                    pool.wait_ge(r_hi_done, s.count(6, i))
                    pool.tensor_tensor(r_split[0:MS[m], 1, :], filtered(m, e), r_split[0:MS[m], 0, :].bitcast(F32),
                                       ALU.subtract).then_inc(r_lo_done, 1)

                main, two = main_live(n), p2.live()
                if main:
                    sig_lo(nxt, 0, 0)
                if two:
                    band_tile(0)
                    band_tile(1)
                if main:
                    rlo(0, 0)
                    sig_lo(nxt, 0, 1)
                    sig_lo(nxt, 1, 0)
                    rlo(0, 1)
                if two:
                    band_tile(2)
                if main:
                    sig_lo(nxt, 1, 1)
                if two:
                    band_tile(3)
                    band_tile(4)
                if main:
                    rlo(0, 2)
                if two:
                    band_tile(5)
                if main:
                    sig_lo(nxt, 2, 0)
                    rlo(1, 0)
                    sig_lo(nxt, 2, 1)
                if two:
                    band_tile(6)
                    band_tile(7)
                if main:
                    rlo(1, 1)
                    rlo(1, 2)

            def prepare():
                pool.wait_ge(group_done, NG * STEPS)
                pool.wait_ge(usum_done, 2 * STEPS)
                pool.wait_ge(sig_lo_done, 6 * (STEPS + 1))
                for t in (v2_hi, v2_lo, v3_hi, v3_lo):
                    pool.memset(t[:, :, :].bitcast(F32), 0.0).then_inc(corners, 1)
                for t in (h1_hi, h1_lo):
                    for e in (0, SH):
                        pool.memset(t[:, :, :, e, :].bitcast(F32), 0.0).then_inc(borders, 1)
                    for e in (0, SW + 1):
                        pool.memset(t[:, :, :, 1:SH, e:e + 1].bitcast(F32), 0.0).then_inc(borders, 1)

            each_step(pool, step, prepare)

            for i in range(H2_DVE, 8):
                pool.wait_ge(h2_hi_done, i + 1)
                pool.tensor_tensor(h2_lo[:, i, :], y[:, i, :], h2_hi[:, i, :].bitcast(F32), ALU.subtract
                                   ).then_inc(h2_lo_pool, 1)

        @block.scalar
        def _(act):
            def copy(dst, src):
                return act.activation(dst, src, ACT.Copy)

            act.wait_ge(prep_pe, 3)
            for kb in range(CB):
                copy(v1pack[:, kb, 0:MID1], psT[:, kb * MID1:(kb + 1) * MID1]).then_inc(v1_hi_done, 1)
            act.wait_ge(masked, 10)
            copy(sel[:, :], self32[:, :]).then_inc(sel_ready, 1)
            act.wait_ge(consts, 7)

            def sig_hi(s, piece, cb):
                if piece != 1:
                    act.wait_ge(diff_done, s.count(4, piece + cb))
                if piece and cb == 0 and s.back:
                    act.wait_ge(group_done, s.ago(1).count(NG, 3 * piece - 1))
                hi, lo, src = signal(s, piece, cb)
                copy(hi, src).then_inc(sig_hi_done, 1)

            for i in range(CB * K):
                cb, v = i // K, i % K
                if SIG0 <= i < SIG0 + 6:
                    act.wait_ge(x_loaded, 32)
                    sig_hi(Step(0, 0), (i - SIG0) // 2, (i - SIG0) % 2)
                act.wait_ge(weff_done, i + 1)
                copy(w_hi[:, cb, v // 2 + 4 * (v % 2), :], psR[i % 2][:, 0:UK]).then_inc(whi_done, 1)
                k = 3 * cb + v // 2
                if v % 2 == 0 and v < K - 1:
                    if k:
                        act.wait_ge(wsum_done, k)
                    copy(wtmp[:, :], psR[i % 2][:, 0:UK]).then_inc(wcopy_done, 1)
                if v % 2 == 1:
                    act.wait_ge(wsum_done, k + 1)
                    copy(w_hi[:, cb, 7 + v // 2, :], wsum[:, :]).then_inc(wsum_hi_done, 1)

            def step(n, q):
                s, p1, p2, p3 = (Step(n, q, d) for d in range(4))
                nxt = Step(n, q, -1)

                def x_out(p, h):
                    act.wait_ge(unit_done, p.count(len(UNITS), 4 if h == 0 else 9))
                    if h == 1:
                        act.wait_ge(y_done, p.count(2, 0))
                    elif p.live(1):
                        act.wait_ge(y_done, p.ago(1).count(2, 1))
                    for cb in range(CB):
                        copy(x1_hi[:, cb, :], psX[cb]).then_inc(x1_hi_done, 1)
                    if h == 1:
                        act.wait_ge(x1_stored[0], p.dma(1, 0))
                    elif p.live(1):
                        act.wait_ge(x1_stored[1], p.ago(1).dma(1, 0))
                    for cb in range(CB):
                        copy(x1[:, cb, :], psX[cb]).then_inc(x1_done, 1)

                def logit(e):
                    act.wait_ge(usum_done, p1.count(2, e))
                    if p1.live(1) and e == 0:
                        act.wait_ge(attn_stored, p2.dma(K, K - 1))
                    act.activation(attn.rearrange("k (r c e) -> k e r c", c=SW // 2, e=2)[:, e],
                                   (psU if e == 0 else psT)[0:KK, :].rearrange("k (r c) -> k r c", c=SW // 2),
                                   ACT.Identity, bias=beff[:, 0:1]).then_inc(logits_done, 1)

                def xT(pair):
                    t = 2 * pair
                    act.wait_ge(xt_done, p2.count(4, pair))
                    wait_slot(act, p2, t + 1)
                    copy(xT_hi[:, t % 4:t % 4 + 2, :], psXT.rearrange("p (t c) -> p t c", c=C)).then_inc(xT_hi_done, 1)

                def bandhi(t):
                    act.wait_ge(band_step, p2.count(NT * K, band_event(t, K - 1)))
                    wait_slot(act, p2, t)
                    copy(band_hi[:, t % 4, :, :], band[:, t % 4, :, :]).then_inc(band_hi_done, 1)

                def mid(m):
                    act.wait_ge(group_done, s.count(NG, m))
                    if p1.live():
                        act.wait_ge(r_lo_done, p1.count(6, 3 + m))
                    copy(middle[0:MS[m], m, :], psR[(m + s.b) % 2][0:MS[m], :]).then_inc(middle_done, 1)

                def rhi(e, m):
                    act.wait_ge(outputs_done, s.count(6, 3 * e + m))
                    i = 3 * e + m
                    if i:
                        act.wait_ge(r_in[(i - 1) // 3], r_events(s, i - 1))
                    elif p1.live():
                        act.wait_ge(r_in[1], r_events(p1, 5))
                    copy(r_split[0:MS[m], 0, :], filtered(m, e)).then_inc(r_hi_done, 1)

                def attn_out(h):
                    act.wait_ge(at_done, p1.count(2, h))
                    copy(attn[:, h * HALF:(h + 1) * HALF], (psT if h == 0 else psU)[0:KK, :]).then_inc(attn_done, 1)

                def yhalf(p, h):
                    act.wait_ge(y_done, p.count(2, h))
                    if p.live(1):
                        act.wait_ge(y1_stored, p.ago(1).dma(1, 0))
                    copy(y1[:, h, :], psU[MID1:P, :]).then_inc(yhalf_done, 1)

                def exponentials():
                    act.wait_ge(sub_done, p1.count(1, 0))
                    act.activation(probs[:, :, :], probs[:, :, :], ACT.Exp).then_inc(exp_done, 1)

                main, two, one, three = main_live(n), p2.live(), p1.live(), p3.live()
                if main:
                    mid(0)
                if three:
                    x_out(p3, 1)
                if two:
                    bandhi(0)
                    xT(0)
                    bandhi(1)
                if one:
                    logit(0)
                if main:
                    mid(1)
                if two:
                    bandhi(2)
                if main:
                    mid(2)
                if two:
                    bandhi(3)
                if main:
                    sig_hi(nxt, 0, 0)
                    rhi(0, 0)
                    sig_hi(nxt, 0, 1)
                if one:
                    logit(1)
                if two:
                    xT(1)
                if main:
                    if q % 2 == 1:
                        act.wait_ge(x_loaded, n * 64 + 32 * ((q + 1) // 2 + 1))
                    sig_hi(nxt, 1, 0)
                    sig_hi(nxt, 1, 1)
                if three:
                    yhalf(p3, 1)
                if one:
                    exponentials()
                if main:
                    rhi(0, 1)
                if two:
                    xT(2)
                    bandhi(4)
                if one:
                    attn_out(0)
                    attn_out(1)
                if main:
                    rhi(0, 2)
                if two:
                    bandhi(5)
                    x_out(p2, 0)
                if main:
                    sig_hi(nxt, 2, 0)
                if two:
                    bandhi(6)
                    xT(3)
                if main:
                    rhi(1, 0)
                    sig_hi(nxt, 2, 1)
                if two:
                    bandhi(7)
                    yhalf(p2, 0)
                if main:
                    rhi(1, 1)
                    rhi(1, 2)

            def prepare():
                act.wait_ge(corners, 4)
                act.wait_ge(vt_done, 2)
                for a in range(2):
                    rows = slice(64 * a, 64 * a + 64)
                    for dst, ty in v2_blocks(v2_hi)[3 * a:3 * a + 3]:
                        copy(dst, v2_of(rows, ty)).then_inc(v_hi_done, 1)
                    copy(v3_hi[rows, a, :], psR[1][rows, C:2 * C]).then_inc(v_hi_done, 1)

            each_step(act, step, prepare)

            def root(i, k):
                act.wait_ge(bn_dve, k)
                act.activation(mv[:, 8:10], mv[:, 6:8], ACT.Sqrt).then_inc(bn_act, 1)

            root(1, BN1_ROOT)
            act.wait_ge(bn_dve, BN1_END)
            act.wait_ge(borders, 8)
            act.wait_ge(y_loaded[0], 16 * (STEPS - LAG + 1))
            for i in range(8):
                if i == 6:
                    act.wait_ge(y_loaded[1], 16 * (LAG - 1))
                act.activation(y[:, i, :], y[:, i, :], ACT.Relu, bias=shift[:, 0:1], scale=scale[:, 0:1]).then_inc(relu1, 1)
                act.wait_ge(relu1, i + 1)
                for a in range(2):
                    copy(h1_part(h1_hi, i, a), y_part(i, a)).then_inc(h1_hi_done, 1)
            act.wait_ge(h1_lo_done, 16)
            for k in range(16):
                act.wait_ge(c2_done, k + 1)
                copy(y[:, k // 2, (k % 2) * HALF:(k % 2 + 1) * HALF], ps[:, k % 8, :]).then_inc(c2_copied, 1)
            root(2, BN2_ROOT)
            act.wait_ge(bn_dve, BN2_END)
            for i in range(8):
                if i == 0:
                    act.wait_ge(c2_copied, 16)
                act.activation(y[:, i, :], y[:, i, :], ACT.Relu, bias=shift[:, 1:2], scale=scale[:, 1:2]).then_inc(relu2, 1)
                act.wait_ge(relu2, i + 1)
                copy(h2_hi[:, i, :], y[:, i, :]).then_inc(h2_hi_done, 1)
            root(3, BN3_ROOT)
            act.wait_ge(bn_dve, BN3_END)
            for u in range(8):
                cb = u % 2
                for k in range(8):
                    h, a, b = k // 4, (k // 2) % 2, k % 2
                    act.wait_ge(f_added, 8 * u + k + 1)
                    if u >= 2 and k % 4 == 0:
                        act.wait_ge(out_stored[u % 2], 16 * (2 * (u // 2 - 1) + 2))
                    act.activation(outs[u % 2][:, 32 * h + a:32 * h + 32:2, b::2],
                                   x1in[:, u % X1_SLOTS, 2 * a + b, h * HALF:(h + 1) * HALF].rearrange("p (r c) -> p r c", c=SW),
                                   ACT.Relu, bias=shift[:, 2 + cb:3 + cb]).then_inc(f_out, 1)

        @block.tensor
        def _(pe):
            def mm3(dst, l_hi, l_lo, r_hi_, r_lo_, first, last, **kw):
                pe.matmul(dst, l_hi, r_hi_, start=first, stop=False, **kw)
                pe.matmul(dst, l_hi, r_lo_, start=False, stop=False, **kw)
                return pe.matmul(dst, l_lo, r_hi_, start=False, stop=last, **kw)

            pe.wait_ge(masked, 10)
            pe.wait_ge(small_loaded, 64)
            pe.transpose(psU[:, 0:KK], w2raw[:, :], ident[0:KK, 0:KK]).then_inc(prep_pe, 1)
            for kb in range(CB):
                pe.transpose(psT[:, kb * MID1:(kb + 1) * MID1], v1raw[:, kb * P:(kb + 1) * P],
                             ident[0:MID1, 0:MID1]).then_inc(prep_pe, 1)
            pe.wait_ge(prep_dve, 1)
            pe.matmul(psXT[0:KK, 0:1], w2T[:, :], b1s[:, :], start=True, stop=True).then_inc(prep_pe, 1)
            for i in range(CB * K):
                kb, v = i // K, i % K
                if v == 0:
                    pe.wait_ge(w1_loaded[kb], 16)
                if i >= 2:
                    pe.wait_ge(wlo_done, i - 1)
                for u in range(K):
                    mm = pe.matmul(psR[i % 2][:, u * KK:(u + 1) * KK], w1raw[:, kb, :, u * K + v], w2T[:, :],
                                   start=True, stop=True)
                mm.then_inc(weff_done, 1)
            pe.wait_ge(wlo_done, CB * K)
            pe.wait_ge(wsum_lo_done, 3 * CB)
            pe.wait_ge(sel_ready, 1)

            def step(n, q):
                s, p1, p2, p3 = (Step(n, q, d) for d in range(4))

                def conv(start, end):
                    for i in range(start, end):
                        g, cb, j = TRIPLES[i]
                        prod, m = GROUPS[g]
                        first, last = (cb, j) == (0, 0), (cb, j) == (CB - 1, TAPS[prod] - 1)
                        if first:
                            if g == 0:
                                pe.wait_ge(sig_lo_done, s.count(6, 3))
                            if g == 3:
                                pe.wait_ge(sig_lo_done, s.count(6, 5))
                            if g in (2, 3, 4):
                                pe.wait_ge(middle_done, s.count(3, g - 2))
                            elif g > 4:
                                pe.wait_ge(outputs_done, s.count(6, g - 5))
                            elif s.live(1):
                                pe.wait_ge(outputs_done, p1.count(6, g + 4))
                        w = weight_of(prod, j)
                        rows = slice(MB * m, MB * m + MS[m])
                        cols = slice(j, j + SW // 2)
                        if prod == ODD:
                            hi, lo = odd_hi[:, s.b, cb, :, cols], odd_lo[:, s.b, cb, :, cols]
                        else:
                            hi, lo = (t[:, cb, :, cols] for t in ((mid_hi, mid_lo) if prod == MIDDLE else (even_hi, even_lo)))
                        mm = mm3(psR[(g + s.b) % 2][0:MS[m], :], w_hi[:, cb, w, rows], w_lo[:, cb, w, rows], hi, lo,
                                 first, last)
                        if last:
                            mm.then_inc(group_done, 1)

                def usum(e):
                    pe.wait_ge(r_in[e], p1.dma(9, 8))
                    if e == 0:
                        if p1.live(2):
                            pe.wait_ge(y1_done, p3.count(2, 0))
                    elif p1.live(1):
                        pe.wait_ge(attn_done, p2.count(2, 0))
                    for m in range(3):
                        at = -MB * m % KK
                        for part in range(2):
                            mm = pe.matmul((psU if e == 0 else psT)[0:KK, :], sel[0:MS[m], at:at + KK],
                                           r_moved[0:MS[m], m, part, e, :],
                                           start=(m == 0 and part == 0), stop=(m == 2 and part == 1))
                    mm.then_inc(usum_done, 1)

                def logits_T():
                    pe.wait_ge(logits_done, p1.count(2, 1))
                    pe.sem_inc(pe_gate, 1)
                    for t in range(NT):
                        mm = pe.transpose(psT[:, t * KK:(t + 1) * KK], attn[:, t * P:(t + 1) * P], ident[0:KK, 0:KK])
                    mm.then_inc(lt_done, 1)

                def attn_T(h):
                    bank = psT if h == 0 else psU
                    pe.wait_ge(probs_done, p1.count(1, 0))
                    if h == 1 and p3.live():
                        pe.wait_ge(y1_done, p3.count(2, 1))
                    pe.sem_inc(pe_gate, 1)
                    for t in range(4):
                        mm = pe.transpose(bank[0:KK, t * P:(t + 1) * P], probs[:, 4 * h + t, :], ident[:, :])
                    mm.then_inc(at_done, 1)

                def band_T(last):
                    if not last:
                        pe.wait_ge(attn_loaded, p2.dma(NT, NT - 1))
                        if p2.live(1):
                            pe.wait_ge(band_step, p3.count(NT * K, band_event(NT - 2, K - 1)))
                        for t in range(NT - 1):
                            mm = pe.transpose(psB[:, t * JV:(t + 1) * JV], attn_jv[:, t, :], ident[0:JV, 0:JV])
                    else:
                        pe.wait_ge(xT_lo_done, p2.count(4, 2))
                        mm = pe.transpose(psXT[:, 0:JV], attn_jv[:, NT - 1, :], ident[0:JV, 0:JV])
                    mm.then_inc(bt_done, 1)

                def x_T(pair):
                    if pair % 2 == 0:
                        pe.wait_ge(xq_loaded[pair // 2], n * 64 + 32 * ((q - 2) // 2 + 1))
                    if pair == 3:
                        pe.wait_ge(band_step, p2.count(NT * K, NT * K - 1))
                    elif pair:
                        pe.wait_ge(xT_lo_done, p2.count(4, pair - 1))
                    elif p2.live(1):
                        pe.wait_ge(xT_lo_done, p3.count(4, 3))
                    for t in range(2):
                        r = 4 * (2 * pair + t)
                        for kb in range(CB):
                            mm = pe.transpose(psXT[:, t * C + kb * P:t * C + (kb + 1) * P],
                                              xq[:, kb, r:r + 4, p2.b::2], ident[:, :])
                    mm.then_inc(xt_done, 1)

                def unit(i):
                    h, t = UNITS[i]
                    first = t == TILES[h][0]
                    if first:
                        if h == 1:
                            pe.wait_ge(x1_lo_done, p2.count(4, 1))
                            pe.wait_ge(x1_done, p2.count(4, 1))
                        elif p2.live(1):
                            pe.wait_ge(x1_lo_done, p3.count(4, 3))
                            pe.wait_ge(x1_done, p3.count(4, 3))
                    pe.wait_ge(band_lo_done, p2.count(NT, t))
                    pe.wait_ge(xT_lo_done, p2.count(4, t // 2))
                    lo, hi = window(h, t)
                    win = slice(lo - (4 * t - PAD), hi - (4 * t - PAD))
                    for cb in range(CB):
                        cols = slice(cb * P, (cb + 1) * P)
                        mm = mm3(psX[cb][:, (lo - HR * h) * SW:(hi - HR * h) * SW],
                                 xT_hi[:, t % 4, cols], xT_lo[:, t % 4, cols],
                                 band_hi[:, t % 4, win, :], band_lo[:, t % 4, win, :],
                                 first, t == TILES[h][-1], skip_group_check=True)
                    mm.then_inc(unit_done, 1)

                def proj(p, h):
                    pe.wait_ge(x1_lo_done, p.count(4, 2 * h + 1))
                    if h == 1:
                        if Step(n, q, 1).live():
                            pe.wait_ge(logits_done, p1.count(2, 0))
                    elif p1.live():
                        pe.wait_ge(attn_done, p1.count(2, 1))
                    if h == 1 or p.live(1):
                        pe.wait_ge(y1_done, p.count(2, h) - 1)
                    for cb in range(CB):
                        for j, r in enumerate((x1_hi, x1_lo)):
                            mm = pe.matmul(psU, v1pack[:, cb, :], r[:, cb, :],
                                           start=(cb == 0 and j == 0), stop=(cb == CB - 1 and j == 1))
                    mm.then_inc(y_done, 1)

                main, two, one, three = main_live(n), p2.live(), p1.live(), p3.live()
                if main:
                    conv(0, 1)
                if two:
                    band_T(False)
                if main:
                    conv(1, 2)
                if two:
                    x_T(0)
                if main:
                    conv(2, 15)
                if one:
                    usum(0)
                if main:
                    conv(15, 21)
                if three:
                    proj(p3, 1)
                if main:
                    conv(21, 32)
                if two:
                    x_T(1)
                if main:
                    conv(32, 34)
                if one:
                    usum(1)
                if main:
                    conv(34, 35)
                if two:
                    unit(0)
                if main:
                    conv(35, 37)
                if one:
                    logits_T()
                if main:
                    conv(37, 40)
                if two:
                    unit(1)
                if main:
                    conv(40, 45)
                if two:
                    x_T(2)
                if one:
                    attn_T(0)
                if main:
                    conv(45, 46)
                if one:
                    attn_T(1)
                if main:
                    conv(46, 47)
                if two:
                    unit(2)
                if main:
                    conv(47, 48)
                if two:
                    band_T(True)
                    unit(3)
                if main:
                    conv(48, 50)
                if two:
                    unit(4)
                if main:
                    conv(50, 58)
                if two:
                    x_T(3)
                if main:
                    conv(58, 59)
                if two:
                    unit(5)
                if main:
                    conv(59, 60)
                if two:
                    unit(6)
                    unit(7)
                    proj(p2, 0)
                if main:
                    conv(60, 66)
                if two:
                    unit(8)
                    unit(9)

            def prepare():
                pe.wait_ge(v_loaded, 16 * 4)
                pe.wait_ge(outputs_done, 6 * STEPS)
                for k in range(2):
                    for t in range(6 - 3 * k):
                        mm = pe.transpose(psR[k][:, t * MID1:(t + 1) * MID1], v2raw[:, :, 6 * k + t::9],
                                          ident[0:MID1, 0:MID1])
                    if k == 1:
                        for cb in range(CB):
                            mm = pe.transpose(psR[1][:, C + cb * P:C + (cb + 1) * P], v3raw[:, cb, :, :], ident[:, :])
                    mm.then_inc(vt_done, 1)

            each_step(pe, step, prepare)

            def average(k, col):
                pe.wait_ge(bn_dve, k)
                pe.matmul(ps[:, 7, 0:1], gavg[:, :], mv[:, col:col + 1], start=True, stop=True).then_inc(bn_pe, 1)

            pe.wait_ge(bn_dve, BN1_STAT)
            pe.matmul(ps[:, 7, 0:2], gavg[0:MID1, :], mv[0:MID1, 0:2], start=True, stop=True).then_inc(bn_pe, 1)
            pe.wait_ge(v_lo_done, 8)
            pe.wait_ge(v_hi_done, 8)
            pe.wait_ge(borders, 8)
            for k in range(16):
                n1, b, h = k // 4, (k // 2) % 2, k % 2
                if k >= 8:
                    pe.wait_ge(c2_copied, k - 7)
                taps = sorted(range(6), key=lambda t: (b + t % 3 - 1) % 2)
                for i, t in enumerate(taps):
                    xb = b + t % 3 - 1
                    if k % 4 == 0:
                        pe.wait_ge(h1_lo_done, 4 * n1 + 2 * (xb % 2) + 2)
                    r0, c0 = HR * h + t // 3, 1 + xb // 2
                    src = n1, xb % 2, slice(r0, r0 + HR), slice(c0, c0 + SW)
                    mm = mm3(ps[:, k % 8, :], v2_hi[:, t, :], v2_lo[:, t, :],
                             h1_hi[:, src[0], src[1], src[2], src[3]], h1_lo[:, src[0], src[1], src[2], src[3]],
                             i == 0, i == 5)
                mm.then_inc(c2_done, 1)
            average(BN2_MEAN, 0)
            average(BN2_VAR, 4)

            def last(k, cb, a, sub, h):
                return mm3(ps[:, k % 8, :], v3_hi[:, a, cb * P:(cb + 1) * P], v3_lo[:, a, cb * P:(cb + 1) * P],
                           h2_hi[:, sub, h * HALF:(h + 1) * HALF], h2_lo[:, sub, h * HALF:(h + 1) * HALF], True, True)

            for k in range(64):
                sub, a, h, cb = k // 8, (k // 4) % 2, (k // 2) % 2, k % 2
                if k % 8 == 0 and sub < H2_DVE:
                    pe.wait_ge(h2_lo_done, sub + 1)
                elif k % 8 == 0:
                    pe.wait_ge(h2_lo_pool, sub - H2_DVE + 1)
                if k >= 8:
                    pe.wait_ge(c3_stat, k - 7)
                last(k, cb, a, sub, h).then_inc(c3_done, 1)
            for k in range(64):
                u, h, a, b = k // 8, (k // 4) % 2, (k // 2) % 2, k % 2
                n1, cb = u // 2, u % 2
                if k < 8:
                    pe.wait_ge(c3_stat, 57 + k)
                else:
                    pe.wait_ge(f_added, k - 7)
                last(k, cb, a, 2 * n1 + b, h).then_inc(f_done, 1)

        @block.vector
        def _(dve):
            def minus(dst, a, b):
                return dve.tensor_tensor(dst, a, b, ALU.subtract)

            dve.wait_ge(prep_pe, 1)
            dve.tensor_copy(w2T[:, :], psU[:, 0:KK]).then_inc(prep_dve, 1)
            dve.wait_ge(v1_hi_done, 2)
            for kb in range(CB):
                minus(v1pack[:, kb, MID1:P], psT[:, kb * MID1:(kb + 1) * MID1],
                      v1pack[:, kb, 0:MID1].bitcast(F32)).then_inc(v1_lo_done, 1)
            dve.wait_ge(prep_pe, 4)
            dve.wait_ge(small_loaded, 64)
            dve.tensor_tensor(beff[:, :], psXT[0:KK, 0:1], b2s[:, :], ALU.add).then_inc(prep_dve, 1)
            dve.wait_ge(masked, 12)
            dve.wait_ge(consts, 7)

            def differences(s, piece, cb):
                i = 2 * piece + cb
                if i:
                    dve.wait_ge(sig_lo_done, s.count(6, 1 if i == 4 else i - 1))
                elif s.live(1):
                    dve.wait_ge(sig_lo_done, s.ago(1).count(6, 5))
                k = 1 if piece == 0 else 0
                width = SIGW[ODD] if piece == 0 else SIGW[EVEN]
                minus(diff[:, :, 0:width], phase(s, cb, k, width), phase(s, cb, k + 1, width)).then_inc(diff_done, 1)

            for i in range(CB * K):
                cb, v = i // K, i % K
                if i - SIG0 in (0, 1, 4, 5):
                    dve.wait_ge(x_loaded, 32)
                    differences(Step(0, 0), (i - SIG0) // 2, (i - SIG0) % 2)
                k = 3 * cb + v // 2
                dve.wait_ge(whi_done, i + 1)
                if v % 2 == 0 and v < K - 1:
                    dve.wait_ge(wcopy_done, k + 1)
                if v % 2 == 1:
                    if k:
                        dve.wait_ge(wsum_hi_done, k)
                        dve.wait_ge(wsum_lo_done, k)
                    dve.tensor_tensor(wsum[:, :], psR[i % 2][:, 0:UK], wtmp[:, :], ALU.add).then_inc(wsum_done, 1)
                w = v // 2 + 4 * (v % 2)
                minus(w_lo[:, cb, w, :], psR[i % 2][:, 0:UK], w_hi[:, cb, w, :].bitcast(F32)).then_inc(wlo_done, 1)
                if v % 2 == 1:
                    dve.wait_ge(wsum_hi_done, k + 1)
                    minus(w_lo[:, cb, 7 + v // 2, :], wsum[:, :], w_hi[:, cb, 7 + v // 2, :].bitcast(F32)
                          ).then_inc(wsum_lo_done, 1)

            def step(n, q):
                s, p1, p2, p3 = (Step(n, q, d) for d in range(4))
                nxt = Step(n, q, -1)

                def x_out(p, h):
                    for cb in range(CB):
                        dve.wait_ge(x1_done, p.count(4, 2 * h + cb))
                        minus(x1_lo[:, cb, :], psX[cb], x1_hi[:, cb, :].bitcast(F32)).then_inc(x1_lo_done, 1)

                def xT(pair):
                    slots = slice(2 * pair % 4, 2 * pair % 4 + 2)
                    dve.wait_ge(xT_hi_done, p2.count(4, pair))
                    wait_slot(dve, p2, 2 * pair + 1)
                    minus(xT_lo[:, slots, :], psXT.rearrange("p (t c) -> p t c", c=C), xT_hi[:, slots, :].bitcast(F32)
                          ).then_inc(xT_lo_done, 1)

                def build_bands(pair):
                    dve.wait_ge(bt_done, p2.count(2, pair // 3))
                    if pair >= 2:
                        dve.wait_ge(band_lo_done, p2.count(NT, 2 * pair - 3))
                    elif p2.live(1):
                        dve.wait_ge(band_lo_done, p3.count(NT, 2 * pair + 5))
                    for v in range(K):
                        for t in (2 * pair, 2 * pair + 1):
                            w = (psB[:, t * JV:(t + 1) * JV] if t < NT - 1 else psXT[:, 0:JV]).rearrange("p (j v) -> p j v", v=K)[:, ::-1, :]
                            if v:
                                dve.wait_ge(band_step, p2.count(NT * K, band_event(t, v - 1)))
                            elif pair or p2.live(1):
                                dve.wait_ge(band_step, p2.count(NT * K, band_event(2 * pair, 0)) - 1)
                            dve.sem_inc(dve_gate, 1)
                            dve.copy_predicated(band[:, t % 4, :, :],
                                                mask[:, v:v + 1, :].bitcast(U32).to_broadcast([P, WIN, SW]),
                                                w[:, :, v:v + 1].to_broadcast([P, WIN, SW])).then_inc(band_step, 1)

                def filter_out(e, m):
                    g = 3 + 3 * e + m
                    dve.wait_ge(group_done, s.count(NG, g))
                    bank = psR[(g + s.b) % 2][0:MS[m], :]
                    if e == 0:
                        dve.wait_ge(middle_done, s.count(3, m))
                        if m:
                            dve.wait_ge(r_lo_done, s.count(6, m - 1))
                        dve.tensor_tensor(evens[0:MS[m], :], bank, middle[0:MS[m], m, :], ALU.add
                                          ).then_inc(outputs_done, 1)
                    else:
                        minus(middle[0:MS[m], m, :], middle[0:MS[m], m, :], bank).then_inc(outputs_done, 1)

                def softmax_top():
                    dve.wait_ge(lt_done, p1.count(1, 0))
                    lt = psT[:, 0:NT * KK].rearrange("p (t k) -> p t k", k=KK)
                    dve.tensor_reduce(smx[:, 0, :], lt, AX_X, ALU.max).then_inc(max_done, 1)
                    dve.wait_ge(max_done, p1.count(1, 0))
                    if p1.live(1):
                        dve.wait_ge(at_done, p2.count(2, 1))
                    minus(probs[:, :, :], lt, smx[:, 0, :].unsqueeze(2).to_broadcast([P, NT, KK])).then_inc(sub_done, 1)

                def softmax_end():
                    dve.wait_ge(exp_done, p1.count(1, 0))
                    dve.tensor_reduce(smx[:, 1, :], probs[:, :, :], AX_X, ALU.add).then_inc(norm_done, 1)
                    dve.wait_ge(norm_done, p1.count(2, 0))
                    dve.reciprocal(smx[:, 2, :], smx[:, 1, :]).then_inc(norm_done, 1)
                    dve.wait_ge(norm_done, p1.count(2, 1))
                    dve.tensor_tensor(probs[:, :, :], probs[:, :, :],
                                      smx[:, 2, :].unsqueeze(2).to_broadcast([P, NT, KK]), ALU.mult
                                      ).then_inc(probs_done, 1)

                def y_out(p, h):
                    dve.wait_ge(yhalf_done, p.count(2, h))
                    dve.tensor_tensor(y1[:, h, :], psU[0:MID1, :], y1[:, h, :], ALU.add).then_inc(y1_done, 1)
                    dve.wait_ge(y1_done, p.count(2, h))
                    dve.bn_stats(stats1[:, p.n * 8 + (2 * p.k + h), :], y1[:, h, :]).then_inc(y1_stat, 1)

                main, two, one, three = main_live(n), p2.live(), p1.live(), p3.live()
                if two:
                    build_bands(0)
                    build_bands(1)
                if three:
                    x_out(p3, 1)
                if main:
                    if q % 2 == 1:
                        dve.wait_ge(x_loaded, n * 64 + 32 * ((q + 1) // 2 + 1))
                    differences(nxt, 0, 0)
                if two:
                    xT(0)
                if main:
                    differences(nxt, 0, 1)
                    filter_out(0, 0)
                if two:
                    build_bands(2)
                if one:
                    softmax_top()
                if main:
                    filter_out(0, 1)
                if two:
                    xT(1)
                if three:
                    y_out(p3, 1)
                if one:
                    softmax_end()
                if two:
                    xT(2)
                if main:
                    differences(nxt, 2, 0)
                    filter_out(0, 2)
                if two:
                    build_bands(3)
                    x_out(p2, 0)
                if main:
                    filter_out(1, 0)
                if two:
                    xT(3)
                if main:
                    differences(nxt, 2, 1)
                    filter_out(1, 1)
                    filter_out(1, 2)
                if two:
                    y_out(p2, 0)

            def prepare():
                dve.wait_ge(v_hi_done, 8)
                for a in range(2):
                    rows = slice(64 * a, 64 * a + 64)
                    for k in range(3 * a, 3 * a + 3):
                        (lo, ty), (hi, _) = v2_blocks(v2_lo)[k], v2_blocks(v2_hi)[k]
                        minus(lo, v2_of(rows, ty), hi.bitcast(F32)).then_inc(v_lo_done, 1)
                    minus(v3_lo[rows, a, :], psR[1][rows, C:2 * C], v3_hi[rows, a, :].bitcast(F32)).then_inc(v_lo_done, 1)

            each_step(dve, step, prepare)

            done = [0]

            def link(op):
                done[0] += 1
                op.then_inc(bn_dve, 1)
                dve.wait_ge(bn_dve, done[0])

            def affine(i, width, var, mean, gamma, beta, roots):
                link(dve.tensor_scalar(mv[:, 6:8], var, EPS, None, ALU.add))
                dve.wait_ge(bn_act, roots)
                sc, sh = scale[:, i:i + width], shift[:, i:i + width]
                link(dve.reciprocal(mv[:, 10:12], mv[:, 8:10]))
                link(dve.tensor_tensor(sc, mv[:, 10:10 + width], gamma, ALU.mult))
                link(dve.tensor_tensor(mv[:, 12:12 + width], mean, sc, ALU.mult))
                link(dve.tensor_tensor(sh, beta, mv[:, 12:12 + width], ALU.subtract))

            def norm(i, pes):
                link(dve.bn_aggr(mv[:, 0:2], stats[:, :, :].rearrange("p k e -> p (k e)")))
                dve.wait_ge(bn_pe, pes)
                link(dve.tensor_copy(mv[:, 2:3], ps[:, 7, 0:1]))
                link(dve.tensor_tensor(mv[:, 3:4], mv[:, 0:1], mv[:, 2:3], ALU.subtract))
                link(dve.scalar_tensor_tensor(out=mv[:, 4:5], in0=mv[:, 3:4], scalar=mv[:, 3:4], in1=mv[:, 1:2],
                                              op0=ALU.mult, op1=ALU.add))
                dve.wait_ge(bn_pe, pes + 1)
                link(dve.tensor_copy(mv[:, 5:6], ps[:, 7, 0:1]))
                affine(i, 1, mv[:, 5:6].to_broadcast([P, 2]), mv[:, 2:3], bn[:, 2 * i:2 * i + 1],
                       bn[:, 2 * i + 1:2 * i + 2], i + 1)

            dve.wait_ge(bn_loaded, 16 * 12)
            dve.wait_ge(y1_stat, 2 * STEPS)
            dve.wait_ge(x1_stored[0], 16 * STEPS)
            dve.wait_ge(x1_stored[1], 16 * STEPS)
            link(dve.bn_aggr(mv[0:MID1, 0:2], stats1[:, :, :].rearrange("p k e -> p (k e)")))
            dve.wait_ge(bn_pe, 1)
            link(dve.tensor_scalar(mv[:, 2:4], ps[:, 7, 0:2], 2.0, None, ALU.mult))
            affine(0, 1, mv[:, 3:4].to_broadcast([P, 2]), mv[:, 2:3], bn[:, 0:1], bn[:, 1:2], 1)
            for i in range(8):
                for a in range(2):
                    dve.wait_ge(h1_hi_done, 2 * i + a + 1)
                    minus(h1_part(h1_lo, i, a), y_part(i, a), h1_part(h1_hi, i, a).bitcast(F32)).then_inc(h1_lo_done, 1)
            for k in range(16):
                dve.wait_ge(c2_copied, k + 1)
                dve.bn_stats(stats[:, k, :], y[:, k // 2, (k % 2) * HALF:(k % 2 + 1) * HALF]).then_inc(c2_stat, 1)
            dve.wait_ge(c2_stat, 16)
            norm(1, 2)
            for i in range(H2_DVE):
                dve.wait_ge(h2_hi_done, i + 1)
                minus(h2_lo[:, i, :], y[:, i, :], h2_hi[:, i, :].bitcast(F32)).then_inc(h2_lo_done, 1)
            for k in range(64):
                dve.wait_ge(c3_done, k + 1)
                dve.bn_stats(stats3[:, k % 2, k // 2, :], ps[:, k % 8, :]).then_inc(c3_stat, 1)
            dve.wait_ge(c3_stat, 64)
            for cb in range(CB):
                link(dve.bn_aggr(mv[:, 2 * cb:2 * cb + 2], stats3[:, cb, :, :].rearrange("p k e -> p (k e)")))
            affine(2, 2, mv[:, 1:4:2], mv[:, 0:4:2], bn[:, 4:6], bn[:, 6:8], 3)
            for k in range(64):
                u, h, sub = k // 8, (k // 4) % 2, k % 4
                cb = u % 2
                if k % 8 == 0:
                    dve.wait_ge(x1_back[u % X1_SLOTS], 16 * (u // X1_SLOTS + 1))
                dve.wait_ge(f_done, k + 1)
                part = x1in[:, u % X1_SLOTS, sub, h * HALF:(h + 1) * HALF]
                dve.scalar_tensor_tensor(out=part, in0=ps[:, k % 8, :], scalar=scale[:, 2 + cb:3 + cb], in1=part,
                                         op0=ALU.mult, op1=ALU.add).then_inc(f_added, 1)


BN1_STAT, BN1_ROOT, BN1_END = 1, 3, 7
BN2_MEAN, BN2_VAR, BN2_ROOT, BN2_END = 8, 11, 13, 17
BN3_ROOT, BN3_END = 20, 24

_INS = ["x", "L0_conv_w1", "L0_conv_b1", "L0_conv_w2", "L0_conv_b2", "L1_conv_w1", "L1_conv_g1", "L1_conv_b1",
        "L1_conv_w2", "L1_conv_g2", "L1_conv_b2", "L1_conv_w3", "L1_conv_g3", "L1_conv_b3"]


def kernel(**inputs):
    import concourse.bacc as bacc
    from concourse.bass_utils import run_bass_kernel_spmd

    nc = bacc.Bacc("TRN2", target_bir_lowering=False, num_devices=1, dynamic_dma_scratch_size=1024)
    arrays, args = {}, []
    for name in _INS:
        a = np.ascontiguousarray(inputs[name])
        arrays[f"in_{name}"] = a
        args.append(nc.dram_tensor(f"in_{name}", a.shape, mybir.dt.from_np(a.dtype), kind="ExternalInput").ap())
    args.append(nc.dram_tensor("out_0", (B, C, H, W), F32, kind="ExternalOutput").ap())
    build(nc, *args)
    r = run_bass_kernel_spmd(nc, [arrays], core_ids=[0])
    return r.results[0]["out_0"]
```
